# Optimizing a Trainium2 kernel written in Bass

```python
import numpy as np
import jax
import jax.numpy as jnp

def _softmax(x, axis=-1):
    return jax.nn.softmax(x, axis=axis)

def _gelu(x):
    return jax.nn.gelu(x, approximate=True)

def _silu(x):
    return jax.nn.silu(x)

def _sigmoid(x):
    return jax.nn.sigmoid(x)

def _layernorm(x, axis=-1, eps=1e-05):
    m = jnp.mean(x, axis=axis, keepdims=True)
    v = jnp.var(x, axis=axis, keepdims=True)
    return (x - m) / jnp.sqrt(v + eps)

def _scatter_add(tgt, idx, src, axis=0):
    return tgt.at[idx].add(src)

def _segment_sum(src, seg, n):
    return jax.ops.segment_sum(src, seg, n)
kernel_name = 'mk_adj_preln_d4_adj_r2_43d3a7'

def setup_inputs(seed: int=0):
    np.random.seed(seed)
    _w = jnp.asarray

    def _rec_inputs():
        import jax
        import jax.numpy as jnp
        _gk = jax.random.key(seed)
        x = -0.0002928 + 1 * jax.random.normal(jax.random.fold_in(_gk, 1), (128, 128, 256), jnp.float32)
        _a = jax.random.bernoulli(jax.random.fold_in(_gk, 2), 0.125, (128, 128))
        _a = jnp.logical_or(_a, jnp.swapaxes(_a, -1, -2))
        _a = jnp.logical_or(_a, jnp.eye(128, dtype=bool))
        _af = _a.astype(jnp.float32)
        adj = _af
        return (x, adj)
    x, adj = _rec_inputs()

    def _L0_gnn_setup():
        import jax, jax.numpy as jnp
        import numpy as np
        B, N, D, H = (4, 1024, 256, 8)
        HD = D // H
        key = jax.random.key(seed)
        ks = jax.random.split(key, 10)
        x = jax.random.normal(ks[0], (B, N, D), dtype=jnp.float32)
        adj = (jax.random.uniform(ks[1], (N, N)) < 0.1).astype(jnp.float32)
        s = 1.0 / np.sqrt(D)
        Wq = jax.random.normal(ks[2], (D, D), dtype=jnp.float32) * s
        Wk = jax.random.normal(ks[3], (D, D), dtype=jnp.float32) * s
        Wv = jax.random.normal(ks[4], (D, D), dtype=jnp.float32) * s
        Wo = jax.random.normal(ks[5], (D, D), dtype=jnp.float32) * s
        bq = jnp.zeros((D,), jnp.float32)
        bk = jnp.zeros((D,), jnp.float32)
        bv = jnp.zeros((D,), jnp.float32)
        bo = jnp.zeros((D,), jnp.float32)
        return {'x': x, 'adj': adj, 'Wq': Wq, 'bq': bq, 'Wk': Wk, 'bk': bk, 'Wv': Wv, 'bv': bv, 'Wo': Wo, 'bo': bo}
    _L0_gnn_all = _L0_gnn_setup()
    _L0_gnn_in = {k: v for k, v in _L0_gnn_all.items() if k in ('Wq', 'bq', 'Wk', 'bk', 'Wv', 'bv', 'Wo', 'bo')}
    del _L0_gnn_all

    def _L1_gnn_setup():
        import jax, jax.numpy as jnp
        import numpy as np
        B, N, D, O = (8, 2048, 256, 256)
        key = jax.random.key(seed)
        k1, k2, k3, k4 = jax.random.split(key, 4)
        x = jax.random.normal(k1, (B, N, D), dtype=jnp.float32)
        adj = jax.random.uniform(k2, (N, N), dtype=jnp.float32)
        weight = jax.random.normal(k3, (D, O), dtype=jnp.float32) * 0.02
        bias = jax.random.normal(k4, (O,), dtype=jnp.float32) * 0.02
        return {'x': x, 'adj': adj, 'weight': weight, 'bias': bias}
    _L1_gnn_all = _L1_gnn_setup()
    _L1_gnn_in = {k: v for k, v in _L1_gnn_all.items() if k in ('weight', 'bias')}
    del _L1_gnn_all

    def _L2_gnn_setup():
        import jax, jax.numpy as jnp
        import numpy as np
        B, N, F_IN, F_OUT = (16, 1024, 256, 256)
        key = jax.random.key(seed)
        k1, k2, k3 = jax.random.split(key, 3)
        x = jax.random.normal(k1, (B, N, F_IN), dtype=jnp.float32)
        adj = jax.random.uniform(k2, (N, N), dtype=jnp.float32)
        bound = np.sqrt(6.0 / F_OUT)
        weight = jax.random.uniform(k3, (F_IN, F_OUT), dtype=jnp.float32, minval=-bound, maxval=bound)
        bias = jnp.zeros((F_OUT,), dtype=jnp.float32)
        return {'x': x, 'adj': adj, 'weight': weight, 'bias': bias}
    _L2_gnn_all = _L2_gnn_setup()
    _L2_gnn_in = {k: v for k, v in _L2_gnn_all.items() if k in ('weight', 'bias')}
    del _L2_gnn_all

    def _L3_gnn_setup():
        import jax, jax.numpy as jnp
        import numpy as np
        key = jax.random.key(seed)
        k1, k2, k3, k4 = jax.random.split(key, 4)
        B, D, N = (4, 128, 256)
        scale = 1.0 / np.sqrt(2 * D)
        x = jax.random.normal(k1, (B, D, N), dtype=jnp.float32)
        W1 = jax.random.normal(k2, (D, D), dtype=jnp.float32) * scale
        W2 = jax.random.normal(k3, (D, D), dtype=jnp.float32) * scale
        b = jax.random.normal(k4, (D,), dtype=jnp.float32) * scale
        return {'x': x, 'W1': W1, 'W2': W2, 'b': b}
    _L3_gnn_all = _L3_gnn_setup()
    _L3_gnn_in = {k: v for k, v in _L3_gnn_all.items() if k in ('b',)}
    del _L3_gnn_all
    return {'x': x, 'adj': adj, 'L0_gnn_Wq': _L0_gnn_in['Wq'], 'L0_gnn_bq': _L0_gnn_in['bq'], 'L0_gnn_Wk': _L0_gnn_in['Wk'], 'L0_gnn_bk': _L0_gnn_in['bk'], 'L0_gnn_Wv': _L0_gnn_in['Wv'], 'L0_gnn_bv': _L0_gnn_in['bv'], 'L0_gnn_Wo': _L0_gnn_in['Wo'], 'L0_gnn_bo': _L0_gnn_in['bo'], 'L1_gnn_weight': _L1_gnn_in['weight'], 'L1_gnn_bias': _L1_gnn_in['bias'], 'L2_gnn_weight': _L2_gnn_in['weight'], 'L2_gnn_bias': _L2_gnn_in['bias'], 'L3_gnn_b': _L3_gnn_in['b']}

def reference(x, adj, L0_gnn_Wq, L0_gnn_bq, L0_gnn_Wk, L0_gnn_bk, L0_gnn_Wv, L0_gnn_bv, L0_gnn_Wo, L0_gnn_bo, L1_gnn_weight, L1_gnn_bias, L2_gnn_weight, L2_gnn_bias, L3_gnn_b):
    import jax
    import jax.numpy as jnp

    def _L0_gnn_ref(x, adj, Wq, bq, Wk, bk, Wv, bv, Wo, bo):
        import jax, jax.numpy as jnp
        import numpy as np
        B, N, D, H = (4, 1024, 256, 8)
        HD = D // H
        b, n, d = x.shape
        q = (x @ Wq + bq).reshape(b, n, H, HD)
        k = (x @ Wk + bk).reshape(b, n, H, HD)
        v = (x @ Wv + bv).reshape(b, n, H, HD)
        scores = jnp.einsum('bqhd,bkhd->bhqk', q, k) / jnp.sqrt(jnp.float32(HD))
        scores = scores + (1.0 - adj)[None, None, :, :] * -1000000000.0
        attn = jax.nn.softmax(scores, axis=-1)
        out = jnp.einsum('bhqk,bkhd->bqhd', attn, v).reshape(b, n, d)
        return out @ Wo + bo

    def _L1_gnn_ref(x, adj, weight, bias):
        import jax, jax.numpy as jnp
        import numpy as np
        B, N, D, O = (8, 2048, 256, 256)
        y = jnp.einsum('nm,bmd->bnd', adj, x)
        out = jnp.einsum('bnd,do->bno', y, weight) + bias
        return out

    def _L2_gnn_ref(x, adj, weight, bias):
        import jax, jax.numpy as jnp
        import numpy as np
        B, N, F_IN, F_OUT = (16, 1024, 256, 256)
        deg = adj.sum(axis=1)
        deg_inv_sqrt = jnp.where(deg > 0, jax.lax.rsqrt(deg), 0.0)
        norm_adj = adj * deg_inv_sqrt[:, None] * deg_inv_sqrt[None, :]
        support = jnp.einsum('bni,io->bno', x, weight)
        output = jnp.einsum('nm,bmo->bno', norm_adj, support)
        return output + bias

    def _L3_gnn_ref(x, W1, W2, b):
        import jax, jax.numpy as jnp
        import numpy as np
        A = jnp.einsum('od,bdn->bon', W1, x)
        C = jnp.einsum('od,bdn->bon', W2, x) + b[None, :, None]
        pre = A[:, :, None, :] + (C - A)[:, :, :, None]
        out = jnp.max(jax.nn.relu(pre), axis=-1)
        return out
    h = jnp.maximum(_layernorm(x, axis=-1), 0.0)
    x = x + _L0_gnn_ref(h, adj, L0_gnn_Wq, L0_gnn_bq, L0_gnn_Wk, L0_gnn_bk, L0_gnn_Wv, L0_gnn_bv, L0_gnn_Wo, L0_gnn_bo)
    h = jnp.maximum(_layernorm(x, axis=-1), 0.0)
    x = x + _L1_gnn_ref(h, adj, L1_gnn_weight, L1_gnn_bias)
    h = jnp.maximum(_layernorm(x, axis=-1), 0.0)
    x = x + _L2_gnn_ref(h, adj, L2_gnn_weight, L2_gnn_bias)
    h = jnp.maximum(_layernorm(x, axis=-1), 0.0)
    x = x + _L3_gnn_ref(h, adj, adj, L3_gnn_b)
    return x

_drawn_inputs = setup_inputs


def setup_inputs(seed=0):
    import zlib

    import numpy as np

    out = dict(_drawn_inputs(seed))
    spreads = {'L0_gnn_bq': (0.0, 2.0),
     'L0_gnn_bk': (0.0, 2.0),
     'L0_gnn_bv': (0.0, 0.376),
     'L0_gnn_bo': (0.0, 0.1),
     'L2_gnn_bias': (0.0, 2.0)}
    factors = {'L0_gnn_Wq': 8.0, 'L0_gnn_Wk': 5.778, 'L1_gnn_bias': 64.0, 'L3_gnn_b': 64.0}
    for name, (base, spread) in spreads.items():
        noise = np.random.default_rng([zlib.crc32(name.encode()), seed]).standard_normal(out[name].shape)
        drawn = base * np.exp(spread * noise) if base else spread * noise
        out[name] = jnp.asarray(drawn.astype(out[name].dtype))
    for name, factor in factors.items():
        out[name] = (out[name] * factor).astype(out[name].dtype)
    return out
```

```python
from contextlib import ExitStack

import concourse.bass as bass
from concourse import mybir

P = 128
D = 256
C = D // P
H = 8
HD = D // H
HC = P // HD
G = 2
W = G * D
VC = HD + 1
OC = HD + 2
EPS = 1e-5
NEG = 1.0e9
TOP = 2.0 ** 14
TINY = 2.0 ** -20
LOWEST = -3.4e38
X_RING = 8
PAR = 2
LAST_LAG = 5
AHEAD = 2

F32 = mybir.dt.float32
F16 = mybir.dt.float16
BF16 = mybir.dt.bfloat16
I32 = mybir.dt.int32
ALU = mybir.AluOpType
ACT = mybir.ActivationFunctionType
X_AXIS = mybir.AxisListType.X
RMAX = bass.bass_isa.ReduceOp.max

WEIGHTS = ("q", "k", "v", "o", "1", "2")
WQ, WK, WV, WO, W1, W2 = range(6)
N_BOUNDS = 10
B_ADJ, B_NORM, B_BQ, B_BK = 6, 7, 8, 9


def build(nc, x, adj, wts, bqk, b3, rows, out):
    B = x.shape[0]
    NG = B // G
    x_g = x.rearrange("(g b) p d -> g p b d", b=G)
    out_g = out.rearrange("(g b) p d -> g p b d", b=G)

    with ExitStack() as ctx:
        def sb(name, shape, dt):
            return ctx.enter_context(nc.sbuf_tensor(name, shape, dt))

        def sem(name):
            return ctx.enter_context(nc.semaphore(name))

        ident = sb("ident", [P, P], F32)
        adj_sb = sb("adj_sb", [P, P], F32)
        mask = sb("mask", [P, P], F32)
        adj_t = sb("adj_t", [P, P], F32)
        adj_ts = sb("adj_ts", [P, P], F32)
        norm_a = sb("norm_a", [P, P], F32)
        norm_t = sb("norm_t", [P, P], F32)
        norm_ts = sb("norm_ts", [P, P], F32)
        w_raw = sb("w_raw", [P, 6, C * D], F32)
        w_hi = [sb(f"w_hi_{n}", [P, C, D], F16) for n in WEIGHTS]
        w_lo = [sb(f"w_lo_{n}", [P, C, D], F16) for n in WEIGHTS]
        bias_qk = sb("bias_qk", [P, 2, C], F32)
        bias_qk_s = sb("bias_qk_s", [P, 2, C], F32)
        bias_v = sb("bias_v", [P, C], F32)
        bias_rows = sb("bias_rows", [1, 3, D], F32)
        row_f = sb("row_f", [1, 3, D], F32)
        row_part = sb("row_part", [1, 3, 3, D], BF16)
        bias_mm = sb("bias_mm", [P, 3, D], BF16)
        ones_mm = sb("ones_mm", [P, P], BF16)
        b3_sb = sb("b3_sb", [P, 1], F32)
        bounds = sb("bounds", [P, 16], F32)
        bound = sb("bound", [P, 16], F32)
        bnd = sb("bnd", [P, 16], F32)
        pow2 = sb("pow2", [P, 16], F32)
        up = sb("up", [P, 16], F32)
        down = sb("down", [P, 16], F32)
        scal = sb("scal", [P, 8], F32)
        C_QK, C_QK_UP, C_0, C_1, C_2 = range(5)
        half = sb("half", [P, G], F32)
        deg = sb("deg", [P, 5], F32)

        X0 = sb("X0", [P, X_RING, W], F32)
        XR = [[sb(f"x{l}_{r}", [P, W], F32) for r in range(PAR)] for l in (1, 2, 3)]
        OUT = [sb(f"outs_{r}", [P, W], F32) for r in range(PAR)]
        HN = [[sb(f"h{l}_{r}", [P, G, D], F32) for r in range(PAR)] for l in range(4)]
        bn = [sb(f"bn{l}", [P, G, 6], F32) for l in range(4)]
        mv = [[sb(f"mv{l}_{r}", [P, G, 2], F32) for r in range(PAR)] for l in range(4)]
        veps = [sb(f"veps{l}", [P, G], F32) for l in range(4)]
        rstd = [[sb(f"rstd{l}_{r}", [P, G], F32) for r in range(PAR)] for l in range(4)]
        mrs = [[sb(f"mrs{l}_{r}", [P, G], F32) for r in range(PAR)] for l in range(4)]
        nmr = [sb(f"nmr{l}", [P, G], F32) for l in range(4)]
        hT_hi = [sb(f"hT_hi_{r}", [P, C, G * P], F16) for r in range(PAR)]
        hT_lo = [sb(f"hT_lo_{r}", [P, C, G * P], F16) for r in range(PAR)]
        q_hi, q_lo, k_hi, k_lo = ([sb(f"{n}_{r}", [P, C, G * P], F16) for r in range(PAR)]
                                  for n in ("q_hi", "q_lo", "k_hi", "k_lo"))
        v_hi = [sb(f"v_hi_{r}", [P, G, H, VC], F16) for r in range(PAR)]
        v_lo = [sb(f"v_lo_{r}", [P, G, H, HD], F16) for r in range(PAR)]
        sm = [sb(f"sm_{b}", [P, H, P], F32) for b in range(G)]
        mx = [sb(f"mx_{b}", [P, H], F32) for b in range(G)]
        ef = [sb(f"ef_{b}", [P, H, P], F32) for b in range(G)]
        eh = [sb(f"eh_{b}", [P, H, P], F16) for b in range(G)]
        el = [sb(f"el_{b}", [P, H, P], F16) for b in range(G)]
        rden = [sb(f"rden_{b}", [P, H], F32) for b in range(G)]
        on = sb("on", [P, G, D], F32)
        oT_hi = sb("oT_hi", [P, C, G * P], F16)
        oT_lo = sb("oT_lo", [P, C, G * P], F16)
        y_hi = [sb(f"y{l}_hi", [P, C, G * P], F16) for l in (1, 2)]
        y_lo = [sb(f"y{l}_lo", [P, C, G * P], F16) for l in (1, 2)]
        amax = sb("amax", [P, G], F32)
        rmax = sb("rmax", [P, G], F32)

        S4 = ctx.enter_context(nc.psum_tensor("S4", [P, HC, G * C, P], F32))
        S_T = S4[:].rearrange("p h n k -> p (h n) k")
        S = [S_T[:, b * H:(b + 1) * H, :] for b in range(G)]
        bank = [ctx.enter_context(nc.psum_tensor(f"bank{n}", [P, W], F32)) for n in range(4)]
        ps_hT = ps_oT = ps_v = ps_y1 = bank[0]
        ps_o0 = ps_q = ps_y2 = bank[1]
        ps_o1 = ps_z0 = ps_z2 = bank[2]
        ps_a = ps_k = ps_z1 = bank[3]
        ps_o = [ps_o0, ps_o1]

        s_setup = sem("setup_loaded")
        s_const = sem("pool_constants")
        s_su = sem("setup_dve")
        s_chain = sem("pool_chain")
        deg_summed, deg_ready, norm_rows = sem("deg_summed"), sem("deg_ready"), sem("norm_rows")
        adj_turned, bv_wo, norm_turned = sem("adj_turned"), sem("bv_wo"), sem("norm_turned")
        maxima_ready, bounds_ready = sem("maxima_ready"), sem("bounds_ready")
        constants = sem("constants_ready")
        x_loaded = [sem(f"x_loaded_{r}") for r in range(PAR)]
        bn_done = [sem(f"bn_done{l}") for l in range(4)]
        mv_done = [sem(f"mv_done{l}") for l in range(4)]
        ve_done = [sem(f"ve_done{l}") for l in range(4)]
        rs_done = [sem(f"rs_done{l}") for l in range(4)]
        mr_done = [sem(f"mr_done{l}") for l in range(4)]
        nm_done = [sem(f"nm_done{l}") for l in range(4)]
        h_done = [sem(f"h_done{l}") for l in range(4)]
        hT_ps, hT_hi_d, hT_lo_d = sem("hT_in_psum"), sem("hT_hi_done"), sem("hT_lo_done")
        q_ps, k_ps, v_ps = sem("q_in_psum"), sem("k_in_psum"), sem("v_in_psum")
        q_hi_d, k_hi_d, v_hi_d = sem("q_hi_done"), sem("k_hi_done"), sem("v_hi_done")
        q_lo_d, k_lo_d, v_lo_d = sem("q_lo_done"), sem("k_lo_done"), sem("v_lo_done")
        s_ps = sem("scores_in_psum")
        sm_d = [sem(f"masked_scores_{b}") for b in range(G)]
        sub_d = [sem(f"max_taken_off_{b}") for b in range(G)]
        sT_ps = [sem(f"scoresT_in_psum_{b}") for b in range(G)]
        ef_d = [sem(f"exp_done_{b}") for b in range(G)]
        eh_d = [sem(f"exp_hi_done_{b}") for b in range(G)]
        el_d = [sem(f"exp_lo_done_{b}") for b in range(G)]
        o_ps = [sem(f"o_in_psum_{b}") for b in range(G)]
        rd_d = [sem(f"rden_done_{b}") for b in range(G)]
        on_d = [sem(f"o_normal_{b}") for b in range(G)]
        oT_ps, oT_hi_d, oT_lo_d = sem("oT_in_psum"), sem("oT_hi_done"), sem("oT_lo_done")
        z_ps = [sem(f"z{l}_in_psum") for l in range(3)]
        x_done = [sem(f"x{l}_done") for l in (1, 2, 3)]
        y_ps = [sem(f"y{l}_in_psum") for l in (1, 2)]
        y_hi_d = [sem(f"y{l}_hi_done") for l in (1, 2)]
        y_lo_d = [sem(f"y{l}_lo_done") for l in (1, 2)]
        a_ps, amax_d, r_d, r0_d, out_d = (sem(n) for n in ("a_in_psum", "amax_done", "relu_done",
                                                           "relu_in_done", "out_done"))
        stored = [sem(f"stored_{r}") for r in range(PAR)]

        def upto(eng, s, i, lag):
            n = i - lag + 1
            if isinstance(n, int):
                n = min(n, NG)
                if n <= 0:
                    return
            eng.wait_ge(s, n)

        def upto_dma(eng, sems, i, lag, par):
            g, r = i - lag, (par - lag) % PAR
            if isinstance(g, int):
                if g >= NG:
                    g -= PAR * ((g - NG) // PAR + 1)
                if g < 0:
                    return
            eng.wait_ge(sems[r], (g - r + 2) * 8)

        def alone(eng, i, *needs):
            if isinstance(i, int):
                for s, lag, *par in needs:
                    (upto_dma if par else upto)(eng, s, i, lag, *par)
                return
            waits = []
            for s, lag, *par in needs:
                r = (par[0] - lag) % PAR if par else None
                n = (i - lag - r + 2) * 8 if par else i - lag + 1
                waits.append((s[r] if par else s, eng.snap(eng.to_reg(n))))
            eng.wait_ge(constants, 1)
            for s, n in waits:
                eng.wait_ge(s, n)

        def live(i, lag):
            return not isinstance(i, int) or 0 <= i - lag < NG

        FIRST = 6
        END = NG - AHEAD
        LAST = NG + LAST_LAG

        def steps(eng, step):
            for i in range(FIRST):
                step(i, i % PAR)
            with eng.Fori(FIRST, END, PAR) as i:
                for r in range(PAR):
                    step(i + r, r)
            for i in range(END, LAST):
                step(i, i % PAR)

        def flat(ap):
            return ap.rearrange("p c n -> p (c n)")

        block = ctx.enter_context(nc.Block())

        @block.sync
        def _(sp):
            sp.dma_start(adj_sb[:], adj).then_inc(s_setup, 16)
            for n in range(6):
                sp.dma_start(w_raw[:, n, :].rearrange("p (c n) -> p c n", c=C),
                             wts[n].rearrange("(c p) n -> p c n", p=P)).then_inc(s_setup, 16)
            sp.dma_start(bias_qk[:], bqk[:, 0:2, :]).then_inc(s_setup, 16)
            sp.dma_start(bias_v[:], bqk[:, 2, :]).then_inc(s_setup, 16)
            sp.dma_start(bias_rows[:], rows).then_inc(s_setup, 16)
            sp.dma_start(b3_sb[:], b3).then_inc(s_setup, 16)

            def load(g, par):
                if isinstance(g, int):
                    src, slot = x_g[g:g + 1], X0[:, g % X_RING, :].unsqueeze(1)
                else:
                    src = x_g[bass.ds(nc.s_assert_within(g, 0, NG - 1), 1)]
                    slot = X0[:, bass.ds(g % X_RING, 1), :]
                sp.dma_start(slot.rearrange("p s (b d) -> p (s b) d", b=G),
                             src.rearrange("g p b d -> p (g b) d")).then_inc(x_loaded[par], 16)

            for g in range(AHEAD):
                load(g, g % PAR)

            def step(i, par):
                if live(i, -AHEAD):
                    alone(sp, i, (mv_done[0], 0), (x_done[0], X_RING - AHEAD))
                    load(i + AHEAD, par)
                r = (par - LAST_LAG) % PAR
                if live(i, LAST_LAG):
                    alone(sp, i, (out_d, LAST_LAG))
                    g = i - LAST_LAG
                    dst = out_g[g:g + 1] if isinstance(g, int) else \
                        out_g[bass.ds(nc.s_assert_within(g, 0, NG - 1), 1)]
                    sp.dma_start(dst.rearrange("g p b d -> p (g b) d"),
                                 OUT[r][:].rearrange("p (b d) -> p b d", b=G)).then_inc(stored[r], 16)

            steps(sp, step)
            upto_dma(sp, stored, NG - 1, 0, (NG - 1) % PAR)
            upto_dma(sp, stored, NG - 2, 0, (NG - 2) % PAR)

        @block.tensor
        def _(pe):
            pe.wait_ge(s_setup, 16 * 11)
            pe.wait_ge(s_const, 3)
            nc.tensor.transpose(bank[0][:, 0:P], adj_sb[:], ident[:]).then_inc(adj_turned, 1)
            for c in range(C):
                mm = nc.tensor.matmul(bank[1][0:1, 0:D], bias_v[:, c:c + 1],
                                      w_raw[:, WO, c * D:(c + 1) * D], start=(c == 0), stop=(c == C - 1))
            mm.then_inc(bv_wo, 1)
            pe.wait_ge(norm_rows, 1)
            nc.tensor.transpose(bank[2][:, 0:P], norm_a[:], ident[:]).then_inc(norm_turned, 1)
            pe.wait_ge(constants, 1)

            def filling(i, s, lag):
                if isinstance(i, int):
                    upto(pe, s, i, lag)

            def thrice(out_ap, a, b, start):
                pairs = [(x_, y_) for c in range(C) for x_, y_ in
                         ((a[0][c], b[0][c]), (a[0][c], b[1][c]), (a[1][c], b[0][c]))]
                for n, (x_, y_) in enumerate(pairs):
                    mm = nc.tensor.matmul(out_ap, x_, y_, start=(start and n == 0),
                                          stop=(n == len(pairs) - 1), skip_group_check=True)
                return mm

            def dense(out_bank, halves, w, bias, s):
                if bias is not None:
                    for b in range(G):
                        nc.tensor.matmul(out_bank[:, b * D:(b + 1) * D], ones_mm[:], bias_mm[:, bias, :],
                                         start=(b == 0), stop=False, skip_group_check=True)
                for b in range(G):
                    t = slice(b * P, (b + 1) * P)
                    mm = thrice(out_bank[:, b * D:(b + 1) * D],
                                [[half_[:, c, t] for c in range(C)] for half_ in halves],
                                [[w_[w][:, c, :] for c in range(C)] for w_ in (w_hi, w_lo)],
                                bias is None)
                mm.then_inc(s, 1)

            def project(out_bank, w, r, s):
                for m in range(C):
                    f = slice(m * P, (m + 1) * P)
                    mm = thrice(out_bank[:, m * G * P:(m + 1) * G * P],
                                [[w_[w][:, c, f] for c in range(C)] for w_ in (w_hi, w_lo)],
                                [[half_[r][:, c, :] for c in range(C)] for half_ in (hT_hi, hT_lo)],
                                True)
                mm.then_inc(s, 1)

            def turn(out_bank, src, s):
                for b in range(G):
                    for c in range(C):
                        o = c * G * P + b * P
                        mm = nc.tensor.transpose(out_bank[:, o:o + P], src[:, b, c * P:(c + 1) * P], ident[:])
                mm.then_inc(s, 1)

            def mix(out_bank, h, a_t, s):
                for b in range(G):
                    for c in range(C):
                        o = c * G * P + b * P
                        mm = nc.tensor.matmul(out_bank[:, o:o + P], h[:, b, c * P:(c + 1) * P], a_t[:],
                                              start=True, stop=True)
                mm.then_inc(s, 1)

            def scores(i, par, b, m):
                if not live(i, 2):
                    return
                if (b, m) == (0, 0):
                    upto(pe, eh_d[1], i, 3)
                    upto(pe, eh_d[0], i, 3)
                    upto(pe, k_lo_d, i, 2)
                    upto(pe, q_lo_d, i, 2)
                t = slice(b * P, (b + 1) * P)
                for n, (q_, k_) in enumerate(((q_hi, k_hi), (q_hi, k_lo), (q_lo, k_hi))):
                    for h in range(HC):
                        f = slice(h * HD, (h + 1) * HD)
                        mm = nc.tensor.matmul(S4[:, h, b * C + m, :], q_[par][f, m, t], k_[par][f, m, t],
                                              start=(n == 0), stop=(n == 2))
                if (b, m) == (G - 1, C - 1):
                    mm.then_inc(s_ps, 1)

            def turn_scores(i, b):
                if live(i, 2):
                    upto(pe, sm_d[1], i, 2)
                    upto(pe, sub_d[b], i, 2)
                    for h in range(H):
                        mm = nc.tensor.transpose(S[b][:, h, :], sm[b][:, h, :], ident[:])
                    mm.then_inc(sT_ps[b], 1)

            def attend(i, r3, b):
                if not live(i, 3):
                    return
                upto(pe, (y_lo_d[1], x_done[2])[b], i - 1, 4)
                filling(i, (q_lo_d, x_done[0])[b], (2, 4)[b])
                upto(pe, v_lo_d, i, 3)
                upto(pe, eh_d[b], i, 3)
                upto(pe, el_d[b], i, 3)
                for h in range(H):
                    o = h * OC
                    nc.tensor.matmul(ps_o[b][:, o:o + VC], eh[b][:, h, :], v_hi[r3][:, b, h, :],
                                     start=True, stop=False)
                    nc.tensor.matmul(ps_o[b][:, o:o + HD], eh[b][:, h, :], v_lo[r3][:, b, h, :],
                                     start=False, stop=False)
                    mm = nc.tensor.matmul(ps_o[b][:, o:o + VC], el[b][:, h, :], v_hi[r3][:, b, h, :],
                                          start=False, stop=True)
                mm.then_inc(o_ps[b], 1)

            def step(i, par):
                r1, r3 = (par - 1) % PAR, (par - 3) % PAR
                r4, r5 = (par - 4) % PAR, (par - 5) % PAR
                if live(i, 1):
                    upto(pe, y_lo_d[0], i - 1, 3)
                    filling(i, v_lo_d, 2)
                    upto(pe, h_done[0], i, 1)
                    turn(ps_hT, HN[0][r1], hT_ps)
                scores(i, par, 0, 0)
                attend(i, r3, 0)
                scores(i, par, 0, 1)
                attend(i, r3, 1)
                scores(i, par, 1, 0)
                if live(i, 5):
                    upto(pe, x_done[1], i - 1, 3)
                    filling(i, k_lo_d, 2)
                    upto(pe, h_done[3], i, 5)
                    nc.tensor.matmul(ps_a[:], adj_t[:], flat(HN[3][r5][:]), start=True,
                                     stop=True).then_inc(a_ps, 1)
                scores(i, par, 1, 1)
                if live(i, 3):
                    upto(pe, hT_lo_d, i, 1)
                    filling(i, y_lo_d[0], 4)
                    upto(pe, on_d[1], i, 3)
                    turn(ps_oT, on, oT_ps)
                if live(i, 1):
                    upto(pe, on_d[0], i, 3)
                    upto(pe, hT_lo_d, i, 1)
                    project(ps_q, WQ, r1, q_ps)
                if live(i, 1):
                    upto(pe, amax_d, i, 5)
                    project(ps_k, WK, r1, k_ps)
                if live(i, 3):
                    upto(pe, on_d[1], i, 3)
                    upto(pe, oT_lo_d, i, 3)
                    dense(ps_z0, (oT_hi, oT_lo), WO, 0, z_ps[0])
                turn_scores(i, 0)
                if live(i, 1):
                    upto(pe, oT_lo_d, i, 3)
                    dense(ps_v, (hT_hi[r1], hT_lo[r1]), WV, None, v_ps)
                if live(i, 4):
                    upto(pe, q_lo_d, i, 1)
                    filling(i, on_d[0], 3)
                    upto(pe, h_done[2], i, 4)
                    mix(ps_y2, HN[2][r4], norm_ts, y_ps[1])
                turn_scores(i, 1)
                if live(i, 3):
                    upto(pe, v_lo_d, i, 1)
                    filling(i, oT_lo_d, 3)
                    upto(pe, h_done[1], i, 3)
                    mix(ps_y1, HN[1][r3], adj_ts, y_ps[0])
                if live(i, 4):
                    upto(pe, x_done[0], i, 3)
                    filling(i, on_d[1], 3)
                    upto(pe, y_lo_d[1], i, 4)
                    dense(ps_z2, (y_hi[1], y_lo[1]), W2, 2, z_ps[2])
                if live(i, 3):
                    upto(pe, k_lo_d, i, 1)
                    filling(i, amax_d, 5)
                    upto(pe, y_lo_d[0], i, 3)
                    dense(ps_z1, (y_hi[0], y_lo[0]), W1, 1, z_ps[1])

            steps(pe, step)

        @block.vector
        def _(dve):
            count = [0]

            def link(ins):
                count[0] += 1
                ins.then_inc(s_su, 1)
                dve.wait_ge(s_su, count[0])

            v = nc.vector
            dve.wait_ge(s_setup, 16 * 11)
            dve.wait_ge(s_const, 3)
            link(v.tensor_reduce(deg[:, 0:1], adj_sb[:], X_AXIS, ALU.add))
            v.tensor_scalar(deg[:, 1:2], deg[:, 0:1], 1e-37, None, ALU.max)
            v.tensor_scalar(deg[:, 2:3], deg[:, 0:1], 0.0, None, ALU.is_gt).then_inc(deg_summed, 1)
            for n in range(6):
                v.tensor_reduce(bounds[:, n:n + 1], w_raw[:, n, :], X_AXIS, ALU.max,
                                apply_absolute_value=True)
            v.tensor_reduce(bounds[:, B_ADJ:B_ADJ + 1], adj_sb[:], X_AXIS, ALU.max, apply_absolute_value=True)
            v.tensor_reduce(bounds[:, B_BQ:B_BQ + 2], bias_qk[:], X_AXIS, ALU.max, apply_absolute_value=True)
            dve.wait_ge(deg_ready, 1)
            v.tensor_scalar(norm_a[:], adj_sb[:], deg[:, 4:5], None, ALU.mult).then_inc(norm_rows, 1)
            dve.wait_ge(norm_turned, 1)
            link(v.tensor_scalar(norm_t[:], bank[2][:, 0:P], deg[:, 4:5], None, ALU.mult))
            v.tensor_reduce(bounds[:, B_NORM:B_NORM + 1], norm_t[:], X_AXIS, ALU.max,
                            apply_absolute_value=True).then_inc(maxima_ready, 1)
            dve.wait_ge(bounds_ready, 1)
            link(v.tensor_scalar(bnd[:, 0:6], bound[:, 0:6], float(D), TINY, ALU.mult, ALU.max))
            link(v.tensor_scalar(bnd[:, 6:8], bound[:, 6:8], 2.0 ** -100, None, ALU.max))
            link(v.tensor_tensor(bnd[:, 0:2], bnd[:, 0:2], bound[:, B_BQ:B_BQ + 2], ALU.add))
            link(v.tensor_scalar(pow2[:, 0:8].bitcast(I32), bnd[:, 0:8].bitcast(I32), 0x7F800000, None,
                                 ALU.bitwise_and))
            link(v.reciprocal(up[:, 0:8], pow2[:, 0:8]))
            link(v.tensor_scalar(up[:, 0:6], up[:, 0:6], TOP, None, ALU.mult))
            link(v.tensor_scalar(down[:, 0:6], pow2[:, 0:6], 1.0 / TOP, None, ALU.mult))
            root = float(HD) ** 0.5
            link(v.scalar_tensor_tensor(scal[:, C_QK:C_QK + 1], down[:, WQ:WQ + 1], 1.0 / root,
                                        down[:, WK:WK + 1], ALU.mult, ALU.mult))
            link(v.scalar_tensor_tensor(scal[:, C_QK_UP:C_QK_UP + 1], up[:, WQ:WQ + 1], root,
                                        up[:, WK:WK + 1], ALU.mult, ALU.mult))
            link(v.tensor_tensor(scal[:, C_0:C_0 + 1], down[:, WV:WV + 1], down[:, WO:WO + 1], ALU.mult))
            link(v.tensor_tensor(scal[:, C_1:C_1 + 1], pow2[:, B_ADJ:B_ADJ + 1], down[:, W1:W1 + 1], ALU.mult))
            link(v.tensor_tensor(scal[:, C_2:C_2 + 1], pow2[:, B_NORM:B_NORM + 1], down[:, W2:W2 + 1], ALU.mult))
            link(v.tensor_tensor(scal[:, 5:6], up[:, WV:WV + 1], up[:, WO:WO + 1], ALU.mult))
            link(v.tensor_tensor(scal[:, 6:7], up[:, B_ADJ:B_ADJ + 1], up[:, W1:W1 + 1], ALU.mult))
            link(v.tensor_tensor(scal[:, 7:8], up[:, B_NORM:B_NORM + 1], up[:, W2:W2 + 1], ALU.mult))
            link(v.tensor_scalar(mask[:], adj_sb[:], 1.0, NEG, ALU.subtract, ALU.mult))
            link(v.tensor_scalar(mask[:], mask[:], scal[:, C_QK_UP:C_QK_UP + 1], None, ALU.mult))
            dve.wait_ge(adj_turned, 1)
            link(v.tensor_copy(adj_t[:], bank[0][:, 0:P]))
            link(v.tensor_scalar(adj_ts[:], adj_t[:], up[:, B_ADJ:B_ADJ + 1], None, ALU.mult))
            link(v.tensor_scalar(norm_ts[:], norm_t[:], up[:, B_NORM:B_NORM + 1], None, ALU.mult))
            for n in range(6):
                w = w_raw[:, n, :]
                hi, lo = flat(w_hi[n][:]), flat(w_lo[n][:])
                link(v.tensor_scalar(hi, w, up[:, n:n + 1], None, ALU.mult))
                link(v.scalar_tensor_tensor(lo, w, up[:, n:n + 1], hi, ALU.mult, ALU.subtract))
            for n in range(2):
                link(v.tensor_scalar(bias_qk_s[:, n, :], bias_qk[:, n, :], up[:, n:n + 1], None, ALU.mult))
            dve.wait_ge(bv_wo, 1)
            link(v.tensor_tensor(bias_rows[:, 0, :], bank[1][0:1, 0:D], bias_rows[:, 0, :], ALU.add))
            for n in range(3):
                row = row_f[:, n, :]
                link(v.tensor_scalar(row, bias_rows[:, n, :], scal[0:1, 5 + n:6 + n], None, ALU.mult))
                for part in range(3):
                    bf = row_part[:, n, part, :]
                    link(v.tensor_copy(bf, row))
                    if part < 2:
                        link(v.tensor_tensor(row, row, bf, ALU.subtract))
                    link(v.tensor_copy(bias_mm[32 * part:32 * part + 1, n, :], bf))
            v.tensor_copy(row_f[:, 0, 0:1], bias_rows[:, 0, 0:1]).then_inc(constants, 1)

            def stats(i, l, lag, src, par):
                if live(i, lag):
                    r = (par - lag) % PAR
                    if l == 0:
                        upto_dma(dve, x_loaded, i, lag, par)
                    else:
                        upto(dve, x_done[l - 1], i, lag)
                    for b in range(G):
                        ins = v.bn_stats(bn[l][:, b, :], src[:, b * D:(b + 1) * D])
                    ins.then_inc(bn_done[l], 1)
                    alone(dve, i, (mr_done[l], lag + PAR), (bn_done[l], lag))
                    for b in range(G):
                        ins = v.bn_aggr(mv[l][r][:, b, :], bn[l][:, b, :])
                    ins.then_inc(mv_done[l], 1)

            def masked(i, b):
                if live(i, 2):
                    alone(dve, i, (s_ps, 2), (sT_ps[b], 3))
                    for h in range(H):
                        ins = v.tensor_tensor_reduce(
                            out=sm[b][:, h, :], in0=S4[:, h % HC, b * C + h // HC, :], in1=mask[:], scale=scal[:, C_QK:C_QK + 1],
                            scalar=LOWEST, op0=ALU.add, op1=ALU.max, accum_out=mx[b][:, h:h + 1])
                    ins.then_inc(sm_d[b], 1)

            def normal(i, b):
                if live(i, 3):
                    upto(dve, o_ps[b], i, 3)
                    o = ps_o[b][:, 0:H * OC].rearrange("p (h e) -> p h e", h=H)
                    v.reciprocal(rden[b][:].unsqueeze(2), o[:, :, HD:HD + 1]).then_inc(rd_d[b], 1)
                    upto(dve, rd_d[b], i, 3)
                    upto(dve, oT_ps, i, 4)
                    v.tensor_tensor(on[:, b, :].rearrange("p (h e) -> p h e", h=H), o[:, :, 0:HD],
                                    rden[b][:].unsqueeze(2).broadcast_to([P, H, HD]),
                                    ALU.mult).then_inc(on_d[b], 1)

            def low(i, lag, psum, hi, lo, hi_done, lo_done, used, used_lag):
                if live(i, lag):
                    upto(dve, hi_done, i, lag)
                    upto(dve, used, i, used_lag)
                    v.tensor_tensor(lo, psum, hi, ALU.subtract).then_inc(lo_done, 1)

            def low_biased(i, lag, psum, n, hi, lo, hi_done, lo_done, par):
                if live(i, lag):
                    r = (par - lag) % PAR
                    upto(dve, hi_done, i, lag)
                    upto(dve, s_ps, i, lag + PAR)
                    for m in range(C):
                        ins = v.scalar_tensor_tensor(
                            lo[r][:, m, :], psum[:, m * G * P:(m + 1) * G * P], bias_qk_s[:, n, m:m + 1],
                            hi[r][:, m, :], ALU.add, ALU.subtract)
                    ins.then_inc(lo_done, 1)

            def residual(i, l, lag, psum, before, par):
                if live(i, lag):
                    r = (par - lag) % PAR
                    upto(dve, z_ps[l], i, lag)
                    upto(dve, h_done[l + 1], i, lag + PAR)
                    if l == 2:
                        upto(dve, out_d, i, lag + PAR)
                    v.scalar_tensor_tensor(XR[l][r][:], psum[:], scal[:, C_0 + l:C_0 + l + 1], before,
                                           ALU.mult, ALU.add).then_inc(x_done[l], 1)

            def x0(i, lag):
                g = i - lag
                return X0[:, g % X_RING, :] if isinstance(g, int) else \
                    X0[:, bass.ds(g % X_RING, 1), :].rearrange("p s n -> p (s n)")

            def step(i, par):
                r1, r3, r4 = (par - 1) % PAR, (par - 3) % PAR, (par - 4) % PAR
                low(i, 1, ps_hT[:], flat(hT_hi[r1][:]), flat(hT_lo[r1][:]), hT_hi_d, hT_lo_d, v_ps, 1 + PAR)
                normal(i, 0)
                normal(i, 1)
                if live(i, 5):
                    upto(dve, a_ps, i, 5)
                    upto(dve, r0_d, i, 6)
                    v.tensor_reduce(amax[:], ps_a[:].rearrange("p (b d) -> p b d", b=G), X_AXIS,
                                    ALU.max).then_inc(amax_d, 1)
                masked(i, 0)
                low(i, 3, ps_oT[:], flat(oT_hi[:]), flat(oT_lo[:]), oT_hi_d, oT_lo_d, z_ps[0], 4)
                low_biased(i, 1, ps_q, 0, q_hi, q_lo, q_hi_d, q_lo_d, par)
                masked(i, 1)
                low_biased(i, 1, ps_k, 1, k_hi, k_lo, k_hi_d, k_lo_d, par)
                residual(i, 0, 3, ps_z0, x0(i, 3) if live(i, 3) else None, par)
                stats(i, 1, 3, XR[0][r3], par)
                if live(i, 0):
                    stats(i, 0, 0, x0(i, 0), par)
                low(i, 1, ps_v[:].rearrange("p (g e) -> p g e", e=HD),
                    v_hi[r1][:].rearrange("p b h e -> p (b h) e")[:, :, 0:HD],
                    v_lo[r1][:].rearrange("p b h e -> p (b h) e"), v_hi_d, v_lo_d, o_ps[1], 1 + PAR)
                low(i, 4, ps_y2[:], flat(y_hi[1][:]), flat(y_lo[1][:]), y_hi_d[1], y_lo_d[1], z_ps[2], 5)
                low(i, 3, ps_y1[:], flat(y_hi[0][:]), flat(y_lo[0][:]), y_hi_d[0], y_lo_d[0], z_ps[1], 4)
                residual(i, 2, 4, ps_z2, XR[1][r4][:], par)
                stats(i, 3, 4, XR[2][r4], par)
                residual(i, 1, 3, ps_z1, XR[0][r3][:], par)
                stats(i, 2, 3, XR[1][r3], par)

            steps(dve, step)

        @block.scalar
        def _(act):
            a = nc.scalar

            def apply(i, l, lag, src, par):
                if live(i, lag):
                    r = (par - lag) % PAR
                    upto(act, mr_done[l], i, lag)
                    upto(act, h_done[l], i, lag + 1)
                    a.activation(nmr[l][:], mrs[l][r][:], ACT.Copy, scale=-1.0).then_inc(nm_done[l], 1)
                    upto(act, nm_done[l], i, lag)
                    upto(act, (hT_ps, y_ps[0], y_ps[1], a_ps)[l], i, lag + PAR)
                    for b in range(G):
                        ins = a.activation(HN[l][r][:, b, :], src[:, b * D:(b + 1) * D], ACT.Relu,
                                           bias=nmr[l][:, b:b + 1], scale=rstd[l][r][:, b:b + 1])
                    ins.then_inc(h_done[l], 1)

            def high(i, lag, in_psum, psum, hi, hi_done, used, used_lag):
                if live(i, lag):
                    upto(act, in_psum, i, lag)
                    upto(act, used, i, used_lag)
                    a.activation(hi, psum, ACT.Copy).then_inc(hi_done, 1)

            def high_biased(i, lag, in_psum, psum, n, hi, hi_done, lo_done, par):
                if live(i, lag):
                    r = (par - lag) % PAR
                    upto(act, in_psum, i, lag)
                    upto(act, lo_done, i, lag + PAR)
                    upto(act, s_ps, i, lag + PAR)
                    for m in range(C):
                        ins = a.activation(hi[r][:, m, :], psum[:, m * G * P:(m + 1) * G * P], ACT.Identity,
                                           bias=bias_qk_s[:, n, m:m + 1])
                    ins.then_inc(hi_done, 1)

            def exponentials(i, b):
                if live(i, 2):
                    upto(act, sT_ps[b], i, 2)
                    upto(act, el_d[b], i, 3)
                    a.activation(ef[b][:], S[b], ACT.Exp).then_inc(ef_d[b], 1)
                    upto(act, o_ps[b], i, 3)
                    a.activation(eh[b][:], S[b], ACT.Exp).then_inc(eh_d[b], 1)

            def x0(i, lag):
                g = i - lag
                return X0[:, g % X_RING, :] if isinstance(g, int) else \
                    X0[:, bass.ds(g % X_RING, 1), :].rearrange("p s n -> p (s n)")

            act.wait_ge(s_const, 4)
            act.wait_ge(constants, 1)

            def step(i, par):
                r1, r3, r4, r5 = (par - 1) % PAR, (par - 3) % PAR, (par - 4) % PAR, (par - 5) % PAR
                high(i, 1, hT_ps, ps_hT[:], flat(hT_hi[r1][:]), hT_hi_d, v_ps, 1 + PAR)
                apply(i, 3, 5, XR[2][r5], par)
                high(i, 3, oT_ps, ps_oT[:], flat(oT_hi[:]), oT_hi_d, z_ps[0], 4)
                apply(i, 2, 4, XR[1][r4], par)
                high_biased(i, 1, q_ps, ps_q, 0, q_hi, q_hi_d, q_lo_d, par)
                high_biased(i, 1, k_ps, ps_k, 1, k_hi, k_hi_d, k_lo_d, par)
                exponentials(i, 0)
                high(i, 1, v_ps, ps_v[:].rearrange("p (g e) -> p g e", e=HD),
                     v_hi[r1][:].rearrange("p b h e -> p (b h) e")[:, :, 0:HD], v_hi_d, o_ps[1], 1 + PAR)
                apply(i, 1, 3, XR[0][r3], par)
                high(i, 4, y_ps[1], ps_y2[:], flat(y_hi[1][:]), y_hi_d[1], z_ps[2], 5)
                exponentials(i, 1)
                high(i, 3, y_ps[0], ps_y1[:], flat(y_hi[0][:]), y_hi_d[0], z_ps[1], 4)
                if live(i, 0):
                    apply(i, 0, 0, x0(i, 0), par)

            steps(act, step)

        @block.gpsimd
        def _(pool):
            g_ = nc.gpsimd
            g_.memset(ident[:], 0.0).then_inc(s_const, 1)
            pool.wait_ge(s_const, 1)
            g_.affine_select(out=ident[:], in_=ident[:], compare_op=ALU.not_equal, fill=1.0, base=0,
                             pattern=[[-1, P]], channel_multiplier=1)
            g_.memset(bounds[:], 0.0)
            g_.memset(ones_mm[:], 1.0)
            g_.memset(half[:], -0.5).then_inc(s_const, 1)
            g_.memset(bias_mm[:], 0.0).then_inc(s_const, 1)
            for r in range(PAR):
                ins = g_.memset(v_hi[r][:], 1.0)
            ins.then_inc(s_const, 1)
            pool.wait_ge(deg_summed, 1)
            pool.wait_ge(s_const, 4)
            g_.tensor_tensor(deg[:, 3:4], deg[:, 1:2], half[:, 0:1], ALU.pow).then_inc(s_chain, 1)
            pool.wait_ge(s_chain, 1)
            g_.tensor_tensor(deg[:, 4:5], deg[:, 3:4], deg[:, 2:3], ALU.mult).then_inc(deg_ready, 1)
            pool.wait_ge(maxima_ready, 1)
            g_.partition_all_reduce(bound[:], bounds[:], P, RMAX).then_inc(bounds_ready, 1)

            def rstds(i, l, lag, par):
                if live(i, lag):
                    r = (par - lag) % PAR
                    alone(pool, i, (mv_done[l], lag))
                    g_.tensor_scalar(veps[l][:].unsqueeze(2), mv[l][r][:, :, 1:2], 1.0, EPS, ALU.mult,
                                     ALU.add).then_inc(ve_done[l], 1)
                    upto(pool, ve_done[l], i, lag)
                    upto(pool, h_done[l], i, lag + PAR)
                    g_.tensor_tensor(rstd[l][r][:], veps[l][:], half[:], ALU.pow).then_inc(rs_done[l], 1)
                    upto(pool, rs_done[l], i, lag)
                    g_.tensor_tensor(mrs[l][r][:].unsqueeze(2), mv[l][r][:, :, 0:1],
                                     rstd[l][r][:].unsqueeze(2), ALU.mult).then_inc(mr_done[l], 1)

            def less_max(i, b):
                if live(i, 2):
                    upto(pool, sm_d[b], i, 2)
                    g_.tensor_tensor(sm[b][:], sm[b][:], mx[b][:].unsqueeze(2).broadcast_to([P, H, P]),
                                     ALU.subtract).then_inc(sub_d[b], 1)

            def exp_low(i, b):
                if live(i, 2):
                    upto(pool, eh_d[b], i, 2)
                    upto(pool, ef_d[b], i, 2)
                    upto(pool, o_ps[b], i, 3)
                    g_.tensor_tensor(el[b][:], ef[b][:], eh[b][:], ALU.subtract).then_inc(el_d[b], 1)

            def last_sum(i, par):
                if live(i, 5):
                    r = (par - 5) % PAR
                    alone(pool, i, (amax_d, 5), (out_d, 6))
                    g_.tensor_scalar(rmax[:], amax[:], b3_sb[:, 0:1], 0.0, ALU.add, ALU.max).then_inc(r0_d, 1)
                    alone(pool, i, (r0_d, 5), (stored, 5 + PAR, par))
                    for b in range(G):
                        ins = g_.tensor_scalar(OUT[r][:, b * D:(b + 1) * D], XR[2][r][:, b * D:(b + 1) * D],
                                               1.0, rmax[:, b:b + 1], ALU.mult, ALU.add)
                    ins.then_inc(out_d, 1)

            def step(i, par):
                rstds(i, 3, 5, par)
                rstds(i, 2, 4, par)
                last_sum(i, par)
                less_max(i, 0)
                less_max(i, 1)
                rstds(i, 1, 3, par)
                exp_low(i, 0)
                rstds(i, 0, 0, par)
                exp_low(i, 1)

            steps(pool, step)


def kernel(**inputs):
    import numpy as _np
    import concourse.bacc as _bacc
    from concourse import mybir as _mybir
    from concourse.bass_utils import run_bass_kernel_spmd as _run

    a = {k: _np.ascontiguousarray(v) for k, v in inputs.items()}
    col = lambda b: b.reshape(C, P).T
    arrays = {"x": a["x"], "adj": a["adj"]}
    for n, k in zip(WEIGHTS, ("L0_gnn_Wq", "L0_gnn_Wk", "L0_gnn_Wv", "L0_gnn_Wo", "L1_gnn_weight",
                              "L2_gnn_weight")):
        arrays[f"w_{n}"] = a[k]
    arrays["bias_cols"] = _np.ascontiguousarray(
        _np.stack([col(a["L0_gnn_bq"]), col(a["L0_gnn_bk"]), col(a["L0_gnn_bv"])], axis=1))
    arrays["bias_3"] = _np.ascontiguousarray(a["L3_gnn_b"].reshape(P, 1))
    arrays["bias_rows"] = _np.ascontiguousarray(
        _np.stack([a["L0_gnn_bo"], a["L1_gnn_bias"], a["L2_gnn_bias"]])[None])
    nc = _bacc.Bacc("TRN2", target_bir_lowering=False, num_devices=1)
    ap = {k: nc.dram_tensor(f"in_{k}", v.shape, _mybir.dt.from_np(v.dtype), kind="ExternalInput").ap()
          for k, v in arrays.items()}
    out = nc.dram_tensor("out_0", a["x"].shape, _mybir.dt.from_np(a["x"].dtype), kind="ExternalOutput").ap()
    build(nc, ap["x"], ap["adj"], [ap[f"w_{n}"] for n in WEIGHTS], ap["bias_cols"], ap["bias_3"],
          ap["bias_rows"], out)
    r = _run(nc, [{f"in_{k}": v for k, v in arrays.items()}], core_ids=[0])
    return r.results[0]["out_0"]
```

```python
from contextlib import ExitStack

import concourse.bass as bass
from concourse import mybir

P = 128
D = 256
C = D // P
H = 8
HD = D // H
HC = P // HD
G = 2
W = G * D
VC = HD + 1
OC = HD + 2
EPS = 1e-5
NEG = 1.0e9
TOP = 2.0 ** 14
TINY = 2.0 ** -20
LOWEST = -3.4e38
X_RING = 8
PAR = 2
AHEAD = 2
LAG = dict(
    bn0=0, ag0=0, rs0=0, ap0=0, hT=1, hTh=1, hTl=1, q=1, qh=1, ql=1, k=1, kh=1, kl=1, v=1, vh=2,
    vl=2, s=2, m0=2, m1=2, lm0=2, lm1=2, ts0=2, ts1=2, ex0=2, ex1=2, el0=2, el1=2, att0=3, att1=3,
    rc0=3, nt0=3, rc1=3, nt1=3, oT=3, oTh=3, oTl=3, z0=3, r0=3, bn1=3, ag1=3, rs1=3, ap1=4, y1=4,
    y1h=4, y1l=4, z1=4, r1=4, bn2=4, ag2=4, rs2=4, ap2=4, y2=4, y2h=4, y2l=4, z2=5, r2=5, bn3=5,
    ag3=5, rs3=5, ap3=5, a=5, mx=5, last=5)
LAST_LAG = max(LAG.values())

F32 = mybir.dt.float32
F16 = mybir.dt.float16
BF16 = mybir.dt.bfloat16
I32 = mybir.dt.int32
ALU = mybir.AluOpType
ACT = mybir.ActivationFunctionType
X_AXIS = mybir.AxisListType.X
RMAX = bass.bass_isa.ReduceOp.max

WEIGHTS = ("q", "k", "v", "o", "1", "2")
WQ, WK, WV, WO, W1, W2 = range(6)
N_BOUNDS = 10
B_ADJ, B_NORM, B_BQ, B_BK = 6, 7, 8, 9


def build(nc, x, adj, wts, bqk, b3, rows, out):
    B = x.shape[0]
    NG = B // G
    x_g = x.rearrange("(g b) p d -> g p b d", b=G)
    out_g = out.rearrange("(g b) p d -> g p b d", b=G)

    with ExitStack() as ctx:
        def sb(name, shape, dt):
            return ctx.enter_context(nc.sbuf_tensor(name, shape, dt))

        def sem(name):
            return ctx.enter_context(nc.semaphore(name))

        ident = sb("ident", [P, P], F32)
        adj_sb = sb("adj_sb", [P, P], F32)
        mask = sb("mask", [P, P], F32)
        adj_t = sb("adj_t", [P, P], F32)
        adj_ts = sb("adj_ts", [P, P], F32)
        norm_a = sb("norm_a", [P, P], F32)
        norm_t = sb("norm_t", [P, P], F32)
        norm_ts = sb("norm_ts", [P, P], F32)
        w_raw = sb("w_raw", [P, 6, C * D], F32)
        w_hi = [sb(f"w_hi_{n}", [P, C, D], F16) for n in WEIGHTS]
        w_lo = [sb(f"w_lo_{n}", [P, C, D], F16) for n in WEIGHTS]
        bias_qk = sb("bias_qk", [P, 2, C], F32)
        bias_qk_s = sb("bias_qk_s", [P, 2, C], F32)
        bias_v = sb("bias_v", [P, C], F32)
        bias_rows = sb("bias_rows", [1, 3, D], F32)
        row_f = sb("row_f", [1, 3, D], F32)
        row_part = sb("row_part", [1, 3, 3, D], BF16)
        bias_mm = sb("bias_mm", [P, 3, D], BF16)
        ones_mm = sb("ones_mm", [P, P], BF16)
        b3_sb = sb("b3_sb", [P, 1], F32)
        bounds = sb("bounds", [P, 16], F32)
        bound = sb("bound", [P, 16], F32)
        bnd = sb("bnd", [P, 16], F32)
        pow2 = sb("pow2", [P, 16], F32)
        up = sb("up", [P, 16], F32)
        down = sb("down", [P, 16], F32)
        scal = sb("scal", [P, 8], F32)
        C_QK, C_QK_UP, C_0, C_1, C_2 = range(5)
        half = sb("half", [P, G], F32)
        deg = sb("deg", [P, 5], F32)

        X0 = sb("X0", [P, X_RING, W], F32)
        XR = [[sb(f"x{l}_{r}", [P, W], F32) for r in range(PAR)] for l in (1, 2, 3)]
        OUT = [sb(f"outs_{r}", [P, W], F32) for r in range(PAR)]
        HN = [[sb(f"h{l}_{r}", [P, G, D], F32) for r in range(PAR)] for l in range(4)]
        bn = [sb(f"bn{l}", [P, G, 6], F32) for l in range(4)]
        mv = [[sb(f"mv{l}_{r}", [P, G, 2], F32) for r in range(PAR)] for l in range(4)]
        veps = [sb(f"veps{l}", [P, G], F32) for l in range(4)]
        rstd = [[sb(f"rstd{l}_{r}", [P, G], F32) for r in range(PAR)] for l in range(4)]
        nmr = [[sb(f"nmr{l}_{r}", [P, G], F32) for r in range(PAR)] for l in range(4)]
        hT_hi = [sb(f"hT_hi_{r}", [P, C, G * P], F16) for r in range(PAR)]
        hT_lo = [sb(f"hT_lo_{r}", [P, C, G * P], F16) for r in range(PAR)]
        q_hi, q_lo, k_hi, k_lo = ([sb(f"{n}_{r}", [P, C, G * P], F16) for r in range(PAR)]
                                  for n in ("q_hi", "q_lo", "k_hi", "k_lo"))
        v_hi = [sb(f"v_hi_{r}", [P, G, H, VC], F16) for r in range(PAR)]
        v_lo = [sb(f"v_lo_{r}", [P, G, H, HD], F16) for r in range(PAR)]
        sm = [sb(f"sm_{b}", [P, H, P], F32) for b in range(G)]
        mx = [sb(f"mx_{b}", [P, H], F32) for b in range(G)]
        ef = [sb(f"ef_{b}", [P, H, P], F32) for b in range(G)]
        eh = [sb(f"eh_{b}", [P, H, P], F16) for b in range(G)]
        el = [sb(f"el_{b}", [P, H, P], F16) for b in range(G)]
        rden = [sb(f"rden_{b}", [P, H], F32) for b in range(G)]
        on = sb("on", [P, G, D], F32)
        oT_hi = sb("oT_hi", [P, C, G * P], F16)
        oT_lo = sb("oT_lo", [P, C, G * P], F16)
        y_hi = [sb(f"y{l}_hi", [P, C, G * P], F16) for l in (1, 2)]
        y_lo = [sb(f"y{l}_lo", [P, C, G * P], F16) for l in (1, 2)]
        amax = sb("amax", [P, G], F32)
        rmax = sb("rmax", [P, G], F32)

        S4 = ctx.enter_context(nc.psum_tensor("S4", [P, HC, G * C, P], F32))
        S_T = S4[:].rearrange("p h n k -> p (h n) k")
        S = [S_T[:, b * H:(b + 1) * H, :] for b in range(G)]
        bank = [ctx.enter_context(nc.psum_tensor(f"bank{n}", [P, W], F32)) for n in range(4)]
        ps_hT, ps_oT, ps_v, ps_y1 = bank[0], bank[2], bank[2], bank[3]
        ps_q, ps_k, ps_y2, ps_a = bank[3], bank[0], bank[1], bank[0]
        ps_z = [bank[2], bank[3], bank[1]]
        ps_o = [bank[1], bank[0]]

        s_setup = sem("setup_loaded")
        s_const = sem("pool_constants")
        s_su = sem("setup_dve")
        s_chain = sem("pool_chain")
        deg_summed, deg_ready, norm_rows = sem("deg_summed"), sem("deg_ready"), sem("norm_rows")
        adj_turned, bv_wo, norm_turned = sem("adj_turned"), sem("bv_wo"), sem("norm_turned")
        maxima_ready, bounds_ready = sem("maxima_ready"), sem("bounds_ready")
        constants = sem("constants_ready")
        x_loaded = [sem(f"x_loaded_{r}") for r in range(PAR)]
        bn_done = [sem(f"bn_done{l}") for l in range(4)]
        mv_done = [sem(f"mv_done{l}") for l in range(4)]
        ve_done = [sem(f"ve_done{l}") for l in range(4)]
        rs_done = [sem(f"rs_done{l}") for l in range(4)]
        nm_done = [sem(f"nm_done{l}") for l in range(4)]
        h_done = [sem(f"h_done{l}") for l in range(4)]
        hT_ps, hT_hi_d, hT_lo_d = sem("hT_in_psum"), sem("hT_hi_done"), sem("hT_lo_done")
        q_ps, k_ps, v_ps = sem("q_in_psum"), sem("k_in_psum"), sem("v_in_psum")
        q_hi_d, k_hi_d, v_hi_d = sem("q_hi_done"), sem("k_hi_done"), sem("v_hi_done")
        q_lo_d, k_lo_d, v_lo_d = sem("q_lo_done"), sem("k_lo_done"), sem("v_lo_done")
        s_ps = sem("scores_in_psum")
        sm_d = [sem(f"masked_scores_{b}") for b in range(G)]
        sub_d = [sem(f"max_taken_off_{b}") for b in range(G)]
        sT_ps = [sem(f"scoresT_in_psum_{b}") for b in range(G)]
        ef_d = [sem(f"exp_done_{b}") for b in range(G)]
        eh_d = [sem(f"exp_hi_done_{b}") for b in range(G)]
        el_d = [sem(f"exp_lo_done_{b}") for b in range(G)]
        o_ps = [sem(f"o_in_psum_{b}") for b in range(G)]
        rd_d = [sem(f"rden_done_{b}") for b in range(G)]
        on_d = [sem(f"o_normal_{b}") for b in range(G)]
        oT_ps, oT_hi_d, oT_lo_d = sem("oT_in_psum"), sem("oT_hi_done"), sem("oT_lo_done")
        z_ps = [sem(f"z{l}_in_psum") for l in range(3)]
        x_done = [sem(f"x{l}_done") for l in (1, 2, 3)]
        y_ps = [sem(f"y{l}_in_psum") for l in (1, 2)]
        y_hi_d = [sem(f"y{l}_hi_done") for l in (1, 2)]
        y_lo_d = [sem(f"y{l}_lo_done") for l in (1, 2)]
        a_ps, amax_d, r_d, r0_d, out_d = (sem(n) for n in ("a_in_psum", "amax_done", "relu_done",
                                                           "relu_in_done", "out_done"))
        stored = [sem(f"stored_{r}") for r in range(PAR)]

        def upto(eng, s, i, lag):
            n = i - lag + 1
            if isinstance(n, int):
                n = min(n, NG)
                if n <= 0:
                    return False
            eng.wait_ge(s, n)
            return True

        def upto_dma(eng, sems, i, lag, par):
            g, r = i - lag, (par - lag) % PAR
            if isinstance(g, int):
                if g >= NG:
                    g -= PAR * ((g - NG) // PAR + 1)
                if g < 0:
                    return
            eng.wait_ge(sems[r], (g - r + 2) * 8)

        def alone(eng, i, *needs):
            if isinstance(i, int):
                for s, lag, *par in needs:
                    (upto_dma if par else upto)(eng, s, i, lag, *par)
                return
            waits = []
            for s, lag, *par in needs:
                r = (par[0] - lag) % PAR if par else None
                n = (i - lag - r + 2) * 8 if par else i - lag + 1
                waits.append((s[r] if par else s, eng.snap(eng.to_reg(n))))
            eng.wait_ge(constants, 1)
            for s, n in waits:
                eng.wait_ge(s, n)

        def live(i, lag):
            return not isinstance(i, int) or 0 <= i - lag < NG

        FIRST = (LAST_LAG + PAR + 1) // PAR * PAR
        END = NG - AHEAD
        LAST = NG + LAST_LAG

        def steps(eng, step):
            for i in range(FIRST):
                step(i, i % PAR)
            with eng.Fori(FIRST, END, PAR) as i:
                for r in range(PAR):
                    step(i + r, r)
            for i in range(END, LAST):
                step(i, i % PAR)

        def flat(ap):
            return ap.rearrange("p c n -> p (c n)")

        block = ctx.enter_context(nc.Block())

        @block.sync
        def _(sp):
            sp.dma_start(adj_sb[:], adj).then_inc(s_setup, 16)
            for n in range(6):
                sp.dma_start(w_raw[:, n, :].rearrange("p (c n) -> p c n", c=C),
                             wts[n].rearrange("(c p) n -> p c n", p=P)).then_inc(s_setup, 16)
            sp.dma_start(bias_qk[:], bqk[:, 0:2, :]).then_inc(s_setup, 16)
            sp.dma_start(bias_v[:], bqk[:, 2, :]).then_inc(s_setup, 16)
            sp.dma_start(bias_rows[:], rows).then_inc(s_setup, 16)
            sp.dma_start(b3_sb[:], b3).then_inc(s_setup, 16)

            def load(g, par):
                if isinstance(g, int):
                    src, slot = x_g[g:g + 1], X0[:, g % X_RING, :].unsqueeze(1)
                else:
                    src = x_g[bass.ds(nc.s_assert_within(g, 0, NG - 1), 1)]
                    slot = X0[:, bass.ds(g % X_RING, 1), :]
                sp.dma_start(slot.rearrange("p s (b d) -> p (s b) d", b=G),
                             src.rearrange("g p b d -> p (g b) d")).then_inc(x_loaded[par], 16)

            for g in range(AHEAD):
                load(g, g % PAR)

            def step(i, par):
                if live(i, -AHEAD):
                    alone(sp, i, (mv_done[0], 0), (x_done[0], X_RING - AHEAD))
                    load(i + AHEAD, par)
                r = (par - LAST_LAG) % PAR
                if live(i, LAST_LAG):
                    alone(sp, i, (out_d, LAST_LAG))
                    g = i - LAST_LAG
                    dst = out_g[g:g + 1] if isinstance(g, int) else \
                        out_g[bass.ds(nc.s_assert_within(g, 0, NG - 1), 1)]
                    sp.dma_start(dst.rearrange("g p b d -> p (g b) d"),
                                 OUT[r][:].rearrange("p (b d) -> p b d", b=G)).then_inc(stored[r], 16)

            steps(sp, step)
            upto_dma(sp, stored, NG - 1, 0, (NG - 1) % PAR)
            upto_dma(sp, stored, NG - 2, 0, (NG - 2) % PAR)

        @block.tensor
        def _(pe):
            pe.wait_ge(s_setup, 16 * 11)
            pe.wait_ge(s_const, 3)
            nc.tensor.transpose(bank[0][:, 0:P], adj_sb[:], ident[:]).then_inc(adj_turned, 1)
            for c in range(C):
                mm = nc.tensor.matmul(bank[1][0:1, 0:D], bias_v[:, c:c + 1],
                                      w_raw[:, WO, c * D:(c + 1) * D], start=(c == 0), stop=(c == C - 1))
            mm.then_inc(bv_wo, 1)
            pe.wait_ge(norm_rows, 1)
            nc.tensor.transpose(bank[2][:, 0:P], norm_a[:], ident[:]).then_inc(norm_turned, 1)
            pe.wait_ge(constants, 1)

            def vacated(i, *tenants):
                for s, lag, back in tenants:
                    if live(i - back, lag):
                        upto(pe, s, i - back, lag)
                        break

            def thrice(out_ap, a, b, start):
                pairs = [(x_, y_) for c in range(C) for x_, y_ in
                         ((a[0][c], b[0][c]), (a[0][c], b[1][c]), (a[1][c], b[0][c]))]
                for n, (x_, y_) in enumerate(pairs):
                    mm = nc.tensor.matmul(out_ap, x_, y_, start=(start and n == 0),
                                          stop=(n == len(pairs) - 1), skip_group_check=True)
                return mm

            def dense(out_bank, halves, w, bias, s):
                if bias is not None:
                    for b in range(G):
                        nc.tensor.matmul(out_bank[:, b * D:(b + 1) * D], ones_mm[:], bias_mm[:, bias, :],
                                         start=(b == 0), stop=False, skip_group_check=True)
                for b in range(G):
                    t = slice(b * P, (b + 1) * P)
                    mm = thrice(out_bank[:, b * D:(b + 1) * D],
                                [[half_[:, c, t] for c in range(C)] for half_ in halves],
                                [[w_[w][:, c, :] for c in range(C)] for w_ in (w_hi, w_lo)],
                                bias is None)
                mm.then_inc(s, 1)

            def project(out_bank, w, r, s):
                for m in range(C):
                    f = slice(m * P, (m + 1) * P)
                    mm = thrice(out_bank[:, m * G * P:(m + 1) * G * P],
                                [[w_[w][:, c, f] for c in range(C)] for w_ in (w_hi, w_lo)],
                                [[half_[r][:, c, :] for c in range(C)] for half_ in (hT_hi, hT_lo)],
                                True)
                mm.then_inc(s, 1)

            def turn(out_bank, src, s):
                for b in range(G):
                    for c in range(C):
                        o = c * G * P + b * P
                        mm = nc.tensor.transpose(out_bank[:, o:o + P], src[:, b, c * P:(c + 1) * P], ident[:])
                mm.then_inc(s, 1)

            def mix(out_bank, h, a_t, s):
                for b in range(G):
                    for c in range(C):
                        o = c * G * P + b * P
                        mm = nc.tensor.matmul(out_bank[:, o:o + P], h[:, b, c * P:(c + 1) * P], a_t[:],
                                              start=True, stop=True)
                mm.then_inc(s, 1)

            def scores(i, par, b, m, first, last):
                lag = LAG["s"]
                if not live(i, lag):
                    return
                r = (par - lag) % PAR
                if first:
                    upto(pe, eh_d[0], i, lag + 1)
                    upto(pe, eh_d[1], i, lag + 1)
                    upto(pe, k_lo_d, i, lag)
                    upto(pe, q_lo_d, i, lag)
                t = slice(b * P, (b + 1) * P)
                for n, (q_, k_) in enumerate(((q_hi, k_hi), (q_hi, k_lo), (q_lo, k_hi))):
                    for h in range(HC):
                        f = slice(h * HD, (h + 1) * HD)
                        mm = nc.tensor.matmul(S4[:, h, b * C + m, :], q_[r][f, m, t], k_[r][f, m, t],
                                              start=(n == 0), stop=(n == 2))
                if last:
                    mm.then_inc(s_ps, 1)

            def turn_scores(i, b):
                lag = LAG[f"ts{b}"]
                if live(i, lag):
                    upto(pe, sm_d[1 - b], i, lag)
                    upto(pe, sub_d[b], i, lag)
                    for h in range(H):
                        mm = nc.tensor.transpose(S[b][:, h, :], sm[b][:, h, :], ident[:])
                    mm.then_inc(sT_ps[b], 1)

            def attend(i, par, b, *tenants):
                lag = LAG[f"att{b}"]
                if not live(i, lag):
                    return
                r = (par - lag) % PAR
                vacated(i, *tenants)
                upto(pe, v_lo_d, i, lag)
                upto(pe, eh_d[b], i, lag)
                upto(pe, el_d[b], i, lag)
                for h in range(H):
                    o = h * OC
                    nc.tensor.matmul(ps_o[b][:, o:o + VC], eh[b][:, h, :], v_hi[r][:, b, h, :],
                                     start=True, stop=False)
                    nc.tensor.matmul(ps_o[b][:, o:o + HD], eh[b][:, h, :], v_lo[r][:, b, h, :],
                                     start=False, stop=False)
                    mm = nc.tensor.matmul(ps_o[b][:, o:o + VC], el[b][:, h, :], v_hi[r][:, b, h, :],
                                          start=False, stop=True)
                mm.then_inc(o_ps[b], 1)

            def h_turned(i, par, *tenants):
                lag = LAG["hT"]
                if live(i, lag):
                    vacated(i, *tenants)
                    upto(pe, h_done[0], i, lag)
                    turn(ps_hT, HN[0][(par - lag) % PAR], hT_ps)

            def q_projected(i, par, *tenants):
                lag = LAG["q"]
                if live(i, lag):
                    vacated(i, *tenants)
                    upto(pe, hT_lo_d, i, lag)
                    project(ps_q, WQ, (par - lag) % PAR, q_ps)

            def k_projected(i, par, *tenants):
                lag = LAG["k"]
                if live(i, lag):
                    vacated(i, *tenants)
                    upto(pe, hT_lo_d, i, lag)
                    project(ps_k, WK, (par - lag) % PAR, k_ps)

            def v_projected(i, par, *tenants):
                lag = LAG["v"]
                if live(i, lag):
                    r = (par - lag) % PAR
                    vacated(i, *tenants)
                    upto(pe, hT_lo_d, i, lag)
                    dense(ps_v, (hT_hi[r], hT_lo[r]), WV, None, v_ps)

            def o_turned(i, par, *tenants):
                lag = LAG["oT"]
                if live(i, lag):
                    vacated(i, *tenants)
                    upto(pe, on_d[0], i, lag)
                    upto(pe, on_d[1], i, lag)
                    turn(ps_oT, on, oT_ps)

            def o_projected(i, par, *tenants):
                lag = LAG["z0"]
                if live(i, lag):
                    vacated(i, *tenants)
                    upto(pe, oT_lo_d, i, lag)
                    dense(ps_z[0], (oT_hi, oT_lo), WO, 0, z_ps[0])

            def h1_mixed(i, par, *tenants):
                lag = LAG["y1"]
                if live(i, lag):
                    vacated(i, *tenants)
                    upto(pe, h_done[1], i, lag)
                    mix(ps_y1, HN[1][(par - lag) % PAR], adj_ts, y_ps[0])

            def y1_projected(i, par, *tenants):
                lag = LAG["z1"]
                if live(i, lag):
                    vacated(i, *tenants)
                    upto(pe, y_lo_d[0], i, lag)
                    dense(ps_z[1], (y_hi[0], y_lo[0]), W1, 1, z_ps[1])

            def h2_mixed(i, par, *tenants):
                lag = LAG["y2"]
                if live(i, lag):
                    vacated(i, *tenants)
                    upto(pe, h_done[2], i, lag)
                    mix(ps_y2, HN[2][(par - lag) % PAR], norm_ts, y_ps[1])

            def y2_projected(i, par, *tenants):
                lag = LAG["z2"]
                if live(i, lag):
                    vacated(i, *tenants)
                    upto(pe, y_lo_d[1], i, lag)
                    dense(ps_z[2], (y_hi[1], y_lo[1]), W2, 2, z_ps[2])

            def layer3(i, par, *tenants):
                lag = LAG["a"]
                if live(i, lag):
                    vacated(i, *tenants)
                    upto(pe, h_done[3], i, lag)
                    nc.tensor.matmul(ps_a[:], adj_t[:], flat(HN[3][(par - lag) % PAR][:]), start=True,
                                     stop=True).then_inc(a_ps, 1)

            def step(i, par):
                y2_projected(i, par, (y_lo_d[1], 4, 1), (on_d[0], 3, 1), (x_done[2], 5, 1))
                h_turned(i, par, (amax_d, 5, 1), (k_lo_d, 1, 1), (on_d[1], 3, 1), (hT_lo_d, 1, 1))
                scores(i, par, 0, 0, first=True, last=False)
                h1_mixed(i, par, (q_lo_d, 1, 1), (x_done[1], 4, 1), (y_lo_d[0], 4, 1))
                scores(i, par, 1, 0, first=False, last=False)
                attend(i, par, 0, (x_done[2], 5, 0), (y_lo_d[1], 4, 1), (on_d[0], 3, 1))
                attend(i, par, 1, (hT_lo_d, 1, 0), (amax_d, 5, 1), (k_lo_d, 1, 1), (on_d[1], 3, 1))
                y1_projected(i, par, (y_lo_d[0], 4, 0), (q_lo_d, 1, 1), (x_done[1], 4, 1))
                o_turned(i, par, (v_lo_d, 1, 1), (x_done[0], 3, 1), (oT_lo_d, 3, 1))
                scores(i, par, 1, 1, first=False, last=False)
                scores(i, par, 0, 1, first=False, last=True)
                k_projected(i, par, (on_d[1], 3, 0), (hT_lo_d, 1, 0), (amax_d, 5, 1),
                            (k_lo_d, 1, 1))
                o_projected(i, par, (oT_lo_d, 3, 0), (v_lo_d, 1, 1), (x_done[0], 3, 1))
                q_projected(i, par, (x_done[1], 4, 0), (y_lo_d[0], 4, 0), (q_lo_d, 1, 1))
                h2_mixed(i, par, (on_d[0], 3, 0), (x_done[2], 5, 0), (y_lo_d[1], 4, 1))
                turn_scores(i, 0)
                v_projected(i, par, (x_done[0], 3, 0), (oT_lo_d, 3, 0), (v_lo_d, 1, 1))
                turn_scores(i, 1)
                layer3(i, par, (k_lo_d, 1, 0), (on_d[1], 3, 0), (hT_lo_d, 1, 0), (amax_d, 5, 1))

            steps(pe, step)

        @block.vector
        def _(dve):
            count = [0]

            def link(ins):
                count[0] += 1
                ins.then_inc(s_su, 1)
                dve.wait_ge(s_su, count[0])

            v = nc.vector
            dve.wait_ge(s_setup, 16 * 11)
            dve.wait_ge(s_const, 3)
            link(v.tensor_reduce(deg[:, 0:1], adj_sb[:], X_AXIS, ALU.add))
            v.tensor_scalar(deg[:, 1:2], deg[:, 0:1], 1e-37, None, ALU.max)
            v.tensor_scalar(deg[:, 2:3], deg[:, 0:1], 0.0, None, ALU.is_gt).then_inc(deg_summed, 1)
            for n in range(6):
                v.tensor_reduce(bounds[:, n:n + 1], w_raw[:, n, :], X_AXIS, ALU.max,
                                apply_absolute_value=True)
            v.tensor_reduce(bounds[:, B_ADJ:B_ADJ + 1], adj_sb[:], X_AXIS, ALU.max, apply_absolute_value=True)
            v.tensor_reduce(bounds[:, B_BQ:B_BQ + 2], bias_qk[:], X_AXIS, ALU.max, apply_absolute_value=True)
            dve.wait_ge(deg_ready, 1)
            v.tensor_scalar(norm_a[:], adj_sb[:], deg[:, 4:5], None, ALU.mult).then_inc(norm_rows, 1)
            dve.wait_ge(norm_turned, 1)
            link(v.tensor_scalar(norm_t[:], bank[2][:, 0:P], deg[:, 4:5], None, ALU.mult))
            v.tensor_reduce(bounds[:, B_NORM:B_NORM + 1], norm_t[:], X_AXIS, ALU.max,
                            apply_absolute_value=True).then_inc(maxima_ready, 1)
            dve.wait_ge(bounds_ready, 1)
            link(v.tensor_scalar(bnd[:, 0:6], bound[:, 0:6], float(D), TINY, ALU.mult, ALU.max))
            link(v.tensor_scalar(bnd[:, 6:8], bound[:, 6:8], 2.0 ** -100, None, ALU.max))
            link(v.tensor_tensor(bnd[:, 0:2], bnd[:, 0:2], bound[:, B_BQ:B_BQ + 2], ALU.add))
            link(v.tensor_scalar(pow2[:, 0:8].bitcast(I32), bnd[:, 0:8].bitcast(I32), 0x7F800000, None,
                                 ALU.bitwise_and))
            link(v.reciprocal(up[:, 0:8], pow2[:, 0:8]))
            link(v.tensor_scalar(up[:, 0:6], up[:, 0:6], TOP, None, ALU.mult))
            link(v.tensor_scalar(down[:, 0:6], pow2[:, 0:6], 1.0 / TOP, None, ALU.mult))
            root = float(HD) ** 0.5
            link(v.scalar_tensor_tensor(scal[:, C_QK:C_QK + 1], down[:, WQ:WQ + 1], 1.0 / root,
                                        down[:, WK:WK + 1], ALU.mult, ALU.mult))
            link(v.scalar_tensor_tensor(scal[:, C_QK_UP:C_QK_UP + 1], up[:, WQ:WQ + 1], root,
                                        up[:, WK:WK + 1], ALU.mult, ALU.mult))
            link(v.tensor_tensor(scal[:, C_0:C_0 + 1], down[:, WV:WV + 1], down[:, WO:WO + 1], ALU.mult))
            link(v.tensor_tensor(scal[:, C_1:C_1 + 1], pow2[:, B_ADJ:B_ADJ + 1], down[:, W1:W1 + 1], ALU.mult))
            link(v.tensor_tensor(scal[:, C_2:C_2 + 1], pow2[:, B_NORM:B_NORM + 1], down[:, W2:W2 + 1], ALU.mult))
            link(v.tensor_tensor(scal[:, 5:6], up[:, WV:WV + 1], up[:, WO:WO + 1], ALU.mult))
            link(v.tensor_tensor(scal[:, 6:7], up[:, B_ADJ:B_ADJ + 1], up[:, W1:W1 + 1], ALU.mult))
            link(v.tensor_tensor(scal[:, 7:8], up[:, B_NORM:B_NORM + 1], up[:, W2:W2 + 1], ALU.mult))
            link(v.tensor_scalar(mask[:], adj_sb[:], 1.0, NEG, ALU.subtract, ALU.mult))
            link(v.tensor_scalar(mask[:], mask[:], scal[:, C_QK_UP:C_QK_UP + 1], None, ALU.mult))
            dve.wait_ge(adj_turned, 1)
            link(v.tensor_copy(adj_t[:], bank[0][:, 0:P]))
            link(v.tensor_scalar(adj_ts[:], adj_t[:], up[:, B_ADJ:B_ADJ + 1], None, ALU.mult))
            link(v.tensor_scalar(norm_ts[:], norm_t[:], up[:, B_NORM:B_NORM + 1], None, ALU.mult))
            for n in range(6):
                w = w_raw[:, n, :]
                hi, lo = flat(w_hi[n][:]), flat(w_lo[n][:])
                link(v.tensor_scalar(hi, w, up[:, n:n + 1], None, ALU.mult))
                link(v.scalar_tensor_tensor(lo, w, up[:, n:n + 1], hi, ALU.mult, ALU.subtract))
            for n in range(2):
                link(v.tensor_scalar(bias_qk_s[:, n, :], bias_qk[:, n, :], up[:, n:n + 1], None, ALU.mult))
            dve.wait_ge(bv_wo, 1)
            link(v.tensor_tensor(bias_rows[:, 0, :], bank[1][0:1, 0:D], bias_rows[:, 0, :], ALU.add))
            for n in range(3):
                row = row_f[:, n, :]
                link(v.tensor_scalar(row, bias_rows[:, n, :], scal[0:1, 5 + n:6 + n], None, ALU.mult))
                for part in range(3):
                    bf = row_part[:, n, part, :]
                    link(v.tensor_copy(bf, row))
                    if part < 2:
                        link(v.tensor_tensor(row, row, bf, ALU.subtract))
                    link(v.tensor_copy(bias_mm[32 * part:32 * part + 1, n, :], bf))
            v.tensor_copy(row_f[:, 0, 0:1], bias_rows[:, 0, 0:1]).then_inc(constants, 1)

            def x_in(i, lag):
                g = i - lag
                return X0[:, g % X_RING, :] if isinstance(g, int) else \
                    X0[:, bass.ds(g % X_RING, 1), :].rearrange("p s n -> p (s n)")

            def moments(i, l, par):
                lag = LAG[f"bn{l}"]
                if live(i, lag):
                    if l == 0:
                        upto_dma(dve, x_loaded, i, lag, par)
                        src = x_in(i, lag)
                    else:
                        upto(dve, x_done[l - 1], i, lag)
                        src = XR[l - 1][(par - lag) % PAR]
                    upto(dve, mv_done[l], i, lag + 1)
                    for b in range(G):
                        ins = v.bn_stats(bn[l][:, b, :], src[:, b * D:(b + 1) * D])
                    ins.then_inc(bn_done[l], 1)

            def gathered(i, l, par):
                lag = LAG[f"ag{l}"]
                if live(i, lag):
                    r = (par - lag) % PAR
                    alone(dve, i, (nm_done[l], lag + PAR), (bn_done[l], lag))
                    for b in range(G):
                        ins = v.bn_aggr(mv[l][r][:, b, :], bn[l][:, b, :])
                    ins.then_inc(mv_done[l], 1)

            def masked(i, b):
                lag = LAG[f"m{b}"]
                if live(i, lag):
                    alone(dve, i, (s_ps, lag), (sT_ps[b], lag + 1))
                    for h in range(H):
                        ins = v.tensor_tensor_reduce(
                            out=sm[b][:, h, :], in0=S4[:, h % HC, b * C + h // HC, :], in1=mask[:],
                            scale=scal[:, C_QK:C_QK + 1], scalar=LOWEST, op0=ALU.add, op1=ALU.max,
                            accum_out=mx[b][:, h:h + 1])
                    ins.then_inc(sm_d[b], 1)

            def outputs(b):
                return ps_o[b][:, 0:H * OC].rearrange("p (h e) -> p h e", h=H)

            def inverse(i, b):
                lag = LAG[f"rc{b}"]
                if live(i, lag):
                    upto(dve, o_ps[b], i, lag)
                    v.reciprocal(rden[b][:].unsqueeze(2), outputs(b)[:, :, HD:HD + 1]).then_inc(rd_d[b], 1)

            def normal(i, b):
                lag = LAG[f"nt{b}"]
                if live(i, lag):
                    upto(dve, rd_d[b], i, lag)
                    upto(dve, oT_ps, i, lag + 1)
                    v.tensor_tensor(on[:, b, :].rearrange("p (h e) -> p h e", h=H), outputs(b)[:, :, 0:HD],
                                    rden[b][:].unsqueeze(2).broadcast_to([P, H, HD]),
                                    ALU.mult).then_inc(on_d[b], 1)

            def low(i, lag, psum, hi, lo, hi_done, lo_done):
                upto(dve, hi_done, i, lag)
                v.tensor_tensor(lo, psum, hi, ALU.subtract).then_inc(lo_done, 1)

            def low_h(i, par):
                lag = LAG["hTl"]
                if live(i, lag):
                    r = (par - lag) % PAR
                    low(i, lag, ps_hT[:], flat(hT_hi[r][:]), flat(hT_lo[r][:]), hT_hi_d, hT_lo_d)

            def low_o(i):
                lag = LAG["oTl"]
                if live(i, lag):
                    low(i, lag, ps_oT[:], flat(oT_hi[:]), flat(oT_lo[:]), oT_hi_d, oT_lo_d)

            def low_v(i, par):
                lag = LAG["vl"]
                if live(i, lag):
                    r = (par - lag) % PAR
                    low(i, lag, ps_v[:].rearrange("p (g e) -> p g e", e=HD),
                        v_hi[r][:].rearrange("p b h e -> p (b h) e")[:, :, 0:HD],
                        v_lo[r][:].rearrange("p b h e -> p (b h) e"), v_hi_d, v_lo_d)

            def low_y(i, l):
                lag = LAG[f"y{l}l"]
                if live(i, lag):
                    low(i, lag, (ps_y1, ps_y2)[l - 1][:], flat(y_hi[l - 1][:]), flat(y_lo[l - 1][:]),
                        y_hi_d[l - 1], y_lo_d[l - 1])

            def low_biased(i, lag, psum, n, hi, lo, hi_done, lo_done, par):
                if live(i, lag):
                    r = (par - lag) % PAR
                    upto(dve, hi_done, i, lag)
                    for m in range(C):
                        ins = v.scalar_tensor_tensor(
                            lo[r][:, m, :], psum[:, m * G * P:(m + 1) * G * P], bias_qk_s[:, n, m:m + 1],
                            hi[r][:, m, :], ALU.add, ALU.subtract)
                    ins.then_inc(lo_done, 1)

            def low_q(i, par):
                low_biased(i, LAG["ql"], ps_q, 0, q_hi, q_lo, q_hi_d, q_lo_d, par)

            def low_k(i, par):
                low_biased(i, LAG["kl"], ps_k, 1, k_hi, k_lo, k_hi_d, k_lo_d, par)

            def residual(i, l, par):
                lag = LAG[f"r{l}"]
                if live(i, lag):
                    r = (par - lag) % PAR
                    before = x_in(i, lag) if l == 0 else XR[l - 1][r][:]
                    upto(dve, z_ps[l], i, lag)
                    upto(dve, h_done[l + 1], i, lag + PAR)
                    if l == 2:
                        upto(dve, out_d, i, lag + PAR)
                    v.scalar_tensor_tensor(XR[l][r][:], ps_z[l][:], scal[:, C_0 + l:C_0 + l + 1], before,
                                           ALU.mult, ALU.add).then_inc(x_done[l], 1)

            def last_max(i):
                lag = LAG["mx"]
                if live(i, lag):
                    upto(dve, a_ps, i, lag)
                    upto(dve, r0_d, i, lag + 1)
                    v.tensor_reduce(amax[:], ps_a[:].rearrange("p (b d) -> p b d", b=G), X_AXIS,
                                    ALU.max).then_inc(amax_d, 1)

            def step(i, par):
                moments(i, 0, par)
                residual(i, 2, par)
                gathered(i, 0, par)
                moments(i, 3, par)
                low_v(i, par)
                low_h(i, par)
                low_y(i, 1)
                inverse(i, 0)
                normal(i, 0)
                inverse(i, 1)
                normal(i, 1)
                gathered(i, 3, par)
                residual(i, 1, par)
                moments(i, 2, par)
                low_o(i)
                gathered(i, 2, par)
                masked(i, 0)
                masked(i, 1)
                residual(i, 0, par)
                moments(i, 1, par)
                gathered(i, 1, par)
                low_k(i, par)
                low_y(i, 2)
                low_q(i, par)
                last_max(i)

            steps(dve, step)

        @block.scalar
        def _(act):
            a = nc.scalar

            def apply(i, l, par):
                lag = LAG[f"ap{l}"]
                if live(i, lag):
                    r = (par - lag) % PAR
                    g = i - lag
                    if l > 0:
                        src = XR[l - 1][r]
                    elif isinstance(g, int):
                        src = X0[:, g % X_RING, :]
                    else:
                        src = X0[:, bass.ds(g % X_RING, 1), :].rearrange("p s n -> p (s n)")
                    upto(act, nm_done[l], i, lag)
                    upto(act, (hT_ps, y_ps[0], y_ps[1], a_ps)[l], i, lag + PAR)
                    for b in range(G):
                        ins = a.activation(HN[l][r][:, b, :], src[:, b * D:(b + 1) * D], ACT.Relu,
                                           bias=nmr[l][r][:, b:b + 1], scale=rstd[l][r][:, b:b + 1])
                    ins.then_inc(h_done[l], 1)

            def high(i, lag, in_psum, psum, hi, hi_done, used, used_lag):
                upto(act, in_psum, i, lag)
                upto(act, used, i, used_lag)
                a.activation(hi, psum, ACT.Copy).then_inc(hi_done, 1)

            def high_h(i, par):
                lag = LAG["hTh"]
                if live(i, lag):
                    high(i, lag, hT_ps, ps_hT[:], flat(hT_hi[(par - lag) % PAR][:]), hT_hi_d,
                         v_ps, lag + PAR)

            def high_o(i):
                lag = LAG["oTh"]
                if live(i, lag):
                    high(i, lag, oT_ps, ps_oT[:], flat(oT_hi[:]), oT_hi_d, z_ps[0], lag + 1)

            def high_v(i, par):
                lag = LAG["vh"]
                if live(i, lag):
                    high(i, lag, v_ps, ps_v[:].rearrange("p (g e) -> p g e", e=HD),
                         v_hi[(par - lag) % PAR][:].rearrange("p b h e -> p (b h) e")[:, :, 0:HD],
                         v_hi_d, o_ps[1], lag + PAR)

            def high_y(i, l):
                lag = LAG[f"y{l}h"]
                if live(i, lag):
                    high(i, lag, y_ps[l - 1], (ps_y1, ps_y2)[l - 1][:], flat(y_hi[l - 1][:]),
                         y_hi_d[l - 1], z_ps[l], lag + 1)

            def high_biased(i, lag, in_psum, psum, n, hi, hi_done, par):
                if live(i, lag):
                    r = (par - lag) % PAR
                    upto(act, in_psum, i, lag)
                    upto(act, s_ps, i, lag + PAR)
                    for m in range(C):
                        ins = a.activation(hi[r][:, m, :], psum[:, m * G * P:(m + 1) * G * P], ACT.Identity,
                                           bias=bias_qk_s[:, n, m:m + 1])
                    ins.then_inc(hi_done, 1)

            def high_q(i, par):
                high_biased(i, LAG["qh"], q_ps, ps_q, 0, q_hi, q_hi_d, par)

            def high_k(i, par):
                high_biased(i, LAG["kh"], k_ps, ps_k, 1, k_hi, k_hi_d, par)

            def exponentials(i, b):
                lag = LAG[f"ex{b}"]
                if live(i, lag):
                    upto(act, sT_ps[b], i, lag)
                    upto(act, el_d[b], i, lag + 1)
                    a.activation(ef[b][:], S[b], ACT.Exp).then_inc(ef_d[b], 1)
                    upto(act, o_ps[b], i, lag + 1)
                    a.activation(eh[b][:], S[b], ACT.Exp).then_inc(eh_d[b], 1)

            act.wait_ge(s_const, 4)
            act.wait_ge(constants, 1)

            def step(i, par):
                apply(i, 1, par)
                high_v(i, par)
                high_h(i, par)
                high_y(i, 1)
                high_o(i)
                apply(i, 0, par)
                apply(i, 3, par)
                apply(i, 2, par)
                high_k(i, par)
                high_y(i, 2)
                high_q(i, par)
                exponentials(i, 0)
                exponentials(i, 1)

            steps(act, step)

        @block.gpsimd
        def _(pool):
            g_ = nc.gpsimd
            g_.memset(ident[:], 0.0).then_inc(s_const, 1)
            pool.wait_ge(s_const, 1)
            g_.affine_select(out=ident[:], in_=ident[:], compare_op=ALU.not_equal, fill=1.0, base=0,
                             pattern=[[-1, P]], channel_multiplier=1)
            g_.memset(bounds[:], 0.0)
            g_.memset(ones_mm[:], 1.0)
            g_.memset(half[:], -0.5).then_inc(s_const, 1)
            g_.memset(bias_mm[:], 0.0).then_inc(s_const, 1)
            for r in range(PAR):
                ins = g_.memset(v_hi[r][:], 1.0)
            ins.then_inc(s_const, 1)
            pool.wait_ge(deg_summed, 1)
            pool.wait_ge(s_const, 4)
            g_.tensor_tensor(deg[:, 3:4], deg[:, 1:2], half[:, 0:1], ALU.pow).then_inc(s_chain, 1)
            pool.wait_ge(s_chain, 1)
            g_.tensor_tensor(deg[:, 4:5], deg[:, 3:4], deg[:, 2:3], ALU.mult).then_inc(deg_ready, 1)
            pool.wait_ge(maxima_ready, 1)
            g_.partition_all_reduce(bound[:], bounds[:], P, RMAX).then_inc(bounds_ready, 1)

            def rstds(i, l, par):
                lag = LAG[f"rs{l}"]
                if live(i, lag):
                    r = (par - lag) % PAR
                    alone(pool, i, (mv_done[l], lag))
                    g_.tensor_scalar(veps[l][:].unsqueeze(2), mv[l][r][:, :, 1:2], 1.0, EPS, ALU.mult,
                                     ALU.add).then_inc(ve_done[l], 1)
                    upto(pool, ve_done[l], i, lag)
                    upto(pool, h_done[l], i, lag + PAR)
                    g_.tensor_tensor(rstd[l][r][:], veps[l][:], half[:], ALU.pow).then_inc(rs_done[l], 1)
                    alone(pool, i, (rs_done[l], lag))
                    for b in range(G):
                        ins = g_.tensor_scalar(nmr[l][r][:, b:b + 1], mv[l][r][:, b, 0:1],
                                               rstd[l][r][:, b:b + 1], -1.0, ALU.mult, ALU.mult)
                    ins.then_inc(nm_done[l], 1)

            def less_max(i, b):
                lag = LAG[f"lm{b}"]
                if live(i, lag):
                    upto(pool, sm_d[b], i, lag)
                    g_.tensor_tensor(sm[b][:], sm[b][:], mx[b][:].unsqueeze(2).broadcast_to([P, H, P]),
                                     ALU.subtract).then_inc(sub_d[b], 1)

            def exp_low(i, b):
                lag = LAG[f"el{b}"]
                if live(i, lag):
                    upto(pool, eh_d[b], i, lag)
                    upto(pool, ef_d[b], i, lag)
                    upto(pool, o_ps[b], i, lag + 1)
                    g_.tensor_tensor(el[b][:], ef[b][:], eh[b][:], ALU.subtract).then_inc(el_d[b], 1)

            def last_sum(i, par):
                lag = LAG["last"]
                if live(i, lag):
                    r = (par - lag) % PAR
                    alone(pool, i, (amax_d, lag), (out_d, lag + 1))
                    g_.tensor_scalar(rmax[:], amax[:], b3_sb[:, 0:1], 0.0, ALU.add, ALU.max).then_inc(r0_d, 1)
                    alone(pool, i, (r0_d, lag), (stored, lag + PAR, par))
                    for b in range(G):
                        ins = g_.tensor_scalar(OUT[r][:, b * D:(b + 1) * D], XR[2][r][:, b * D:(b + 1) * D],
                                               1.0, rmax[:, b:b + 1], ALU.mult, ALU.add)
                    ins.then_inc(out_d, 1)

            def step(i, par):
                rstds(i, 0, par)
                rstds(i, 3, par)
                rstds(i, 2, par)
                less_max(i, 0)
                less_max(i, 1)
                rstds(i, 1, par)
                exp_low(i, 0)
                exp_low(i, 1)
                last_sum(i, par)

            steps(pool, step)


def kernel(**inputs):
    import numpy as _np
    import concourse.bacc as _bacc
    from concourse import mybir as _mybir
    from concourse.bass_utils import run_bass_kernel_spmd as _run

    a = {k: _np.ascontiguousarray(v) for k, v in inputs.items()}
    col = lambda b: b.reshape(C, P).T
    arrays = {"x": a["x"], "adj": a["adj"]}
    for n, k in zip(WEIGHTS, ("L0_gnn_Wq", "L0_gnn_Wk", "L0_gnn_Wv", "L0_gnn_Wo", "L1_gnn_weight",
                              "L2_gnn_weight")):
        arrays[f"w_{n}"] = a[k]
    arrays["bias_cols"] = _np.ascontiguousarray(
        _np.stack([col(a["L0_gnn_bq"]), col(a["L0_gnn_bk"]), col(a["L0_gnn_bv"])], axis=1))
    arrays["bias_3"] = _np.ascontiguousarray(a["L3_gnn_b"].reshape(P, 1))
    arrays["bias_rows"] = _np.ascontiguousarray(
        _np.stack([a["L0_gnn_bo"], a["L1_gnn_bias"], a["L2_gnn_bias"]])[None])
    nc = _bacc.Bacc("TRN2", target_bir_lowering=False, num_devices=1)
    ap = {k: nc.dram_tensor(f"in_{k}", v.shape, _mybir.dt.from_np(v.dtype), kind="ExternalInput").ap()
          for k, v in arrays.items()}
    out = nc.dram_tensor("out_0", a["x"].shape, _mybir.dt.from_np(a["x"].dtype), kind="ExternalOutput").ap()
    build(nc, ap["x"], ap["adj"], [ap[f"w_{n}"] for n in WEIGHTS], ap["bias_cols"], ap["bias_3"],
          ap["bias_rows"], out)
    r = _run(nc, [{f"in_{k}": v for k, v in arrays.items()}], core_ids=[0])
    return r.results[0]["out_0"]
```

```python
from contextlib import ExitStack

import concourse.bass as bass
from concourse import mybir

P = 128
D = 256
C = D // P
H = 8
HD = D // H
HC = P // HD
G = 2
W = G * D
VC = HD + 1
OC = HD + 2
EPS = 1e-5
NEG = 1.0e9
TOP = 2.0 ** 14
TINY = 2.0 ** -20
LOWEST = -3.4e38
X_RING = 8
PAR = 2
AHEAD = 2
LAG = dict(
    bn0=0, ag0=0, ve0=0, pw0=1, nm0=1, xb0=3, ap0=1, hT=2, hTh=2, hTl=2, q=2, qh=3, ql=3, k=2, kh=3,
    kl=3, v=2, vh=3, vl=3, s=3, m0=4, m1=3, lm0=4, lm1=4, ts0=4, ts1=4, ex0=4, ex1=4, el0=4, el1=4,
    att0=4, att1=4, rc0=4, nt0=4, rc1=4, nt1=4, oT=5, oTh=5, oTl=5, z0=5, r0=5, bn1=5, ag1=5, ve1=5,
    pw1=5, nm1=6, xb1=5, ap1=6, y1=6, y1h=6, y1l=6, z1=6, r1=6, bn2=6, ag2=6, ve2=6, pw2=7, nm2=7,
    xb2=6, ap2=7, y2=7, y2h=7, y2l=8, z2=8, r2=8, bn3=8, ag3=8, ve3=8, pw3=8, nm3=9, ap3=9, a=9,
    mx=9, rm=9, last=9)
LAST_LAG = max(LAG.values())

F32 = mybir.dt.float32
F16 = mybir.dt.float16
I32 = mybir.dt.int32
ALU = mybir.AluOpType
ACT = mybir.ActivationFunctionType
X_AXIS = mybir.AxisListType.X
RMAX = bass.bass_isa.ReduceOp.max

WEIGHTS = ("q", "k", "v", "o", "1", "2")
WQ, WK, WV, WO, W1, W2 = range(6)


def build(nc, x, adj, wts, bqk, b3, rows, out):
    B = x.shape[0]
    NG = B // G
    x_g = x.rearrange("(g b) p d -> g p b d", b=G)
    out_g = out.rearrange("(g b) p d -> g p b d", b=G)

    with ExitStack() as ctx:
        def sb(name, shape, dt):
            return ctx.enter_context(nc.sbuf_tensor(name, shape, dt))

        def sem(name):
            return ctx.enter_context(nc.semaphore(name))

        ident = sb("ident", [P, P], F32)
        adj_sb = sb("adj_sb", [P, P], F32)
        mask = sb("mask", [P, P], F32)
        adj_t = sb("adj_t", [P, P], F32)
        adj_ts = sb("adj_ts", [P, P], F32)
        norm_a = sb("norm_a", [P, P], F32)
        norm_t = sb("norm_t", [P, P], F32)
        norm_ts = sb("norm_ts", [P, P], F32)
        w_raw = sb("w_raw", [P, 6, C * D], F32)
        w_hi = [sb(f"w_hi_{n}", [P, C, D], F16) for n in WEIGHTS]
        w_lo = [sb(f"w_lo_{n}", [P, C, D], F16) for n in WEIGHTS]
        bias_qk = sb("bias_qk", [P, 2, C], F32)
        bias_qk_s = sb("bias_qk_s", [P, 2, C], F32)
        bias_v = sb("bias_v", [P, C], F32)
        bv_wide = sb("bv_wide", [P, C, P], F32)
        ones = sb("ones", [P, P], F32)
        bias_row = sb("bias_row", [P, 3, D], F32)
        bias = sb("bias", [P, 3, D], F32)
        b3_sb = sb("b3_sb", [P, 1], F32)
        bounds, bound, bnd, pow2, up, down = (
            [sb(f"{n}_{part}", [P, 5], F32) for part in range(2)]
            for n in ("bounds", "bound", "bnd", "pow2", "up", "down"))
        scal = sb("scal", [P, 5], F32)
        C_QK, C_QK_UP, C_0, C_1, C_2 = range(5)
        deg = sb("deg", [P, 4], F32)
        half = sb("half", [P, G], F32)
        table_in = sb("table_in", [P, 1], F32)
        mark = sb("mark", [P, 4], F32)

        X0 = sb("X0", [P, X_RING, W], F32)
        XR = [[sb(f"x{l}_{r}", [P, W], F32) for r in range(PAR)] for l in (1, 2, 3)]
        OUT = [sb(f"outs_{r}", [P, W], F32) for r in range(PAR)]
        HN = [[sb(f"h{l}_{r}", [P, G, D], F32) for r in range(PAR)] for l in range(4)]
        XB = [[sb(f"xb{l}_{r}", [P, G, D], F32) for r in range(PAR)] for l in range(3)]
        bn = [sb(f"bn{l}", [P, G, 6], F32) for l in range(4)]
        mv = [[sb(f"mv{l}_{r}", [P, G, 2], F32) for r in range(PAR)] for l in range(4)]
        veps = [[sb(f"veps{l}_{r}", [P, G], F32) for r in range(PAR)] for l in range(4)]
        rstd = [[sb(f"rstd{l}_{r}", [P, G], F32) for r in range(PAR)] for l in range(4)]
        nmr = [[sb(f"nmr{l}_{r}", [P, G], F32) for r in range(PAR)] for l in range(4)]
        hT_hi = [sb(f"hT_hi_{r}", [P, C, G * P], F16) for r in range(PAR)]
        hT_lo = [sb(f"hT_lo_{r}", [P, C, G * P], F16) for r in range(PAR)]
        q_hi, q_lo, k_hi, k_lo = ([sb(f"{n}_{r}", [P, C, G * P], F16) for r in range(PAR)]
                                  for n in ("q_hi", "q_lo", "k_hi", "k_lo"))
        v_hi = [sb(f"v_hi_{r}", [P, G, H, VC], F16) for r in range(PAR)]
        v_lo = [sb(f"v_lo_{r}", [P, G, H, HD], F16) for r in range(PAR)]
        sm = [sb(f"sm_{b}", [P, H, P], F32) for b in range(G)]
        mx = [sb(f"mx_{b}", [P, H], F32) for b in range(G)]
        ef = [sb(f"ef_{b}", [P, H, P], F32) for b in range(G)]
        eh = [sb(f"eh_{b}", [P, H, P], F16) for b in range(G)]
        el = [sb(f"el_{b}", [P, H, P], F16) for b in range(G)]
        rden = [sb(f"rden_{b}", [P, H], F32) for b in range(G)]
        on = sb("on", [P, G, D], F32)
        oT_hi = sb("oT_hi", [P, C, G * P], F16)
        oT_lo = sb("oT_lo", [P, C, G * P], F16)
        y_hi = [sb(f"y{l}_hi", [P, C, G * P], F16) for l in (1, 2)]
        y_lo = [sb(f"y{l}_lo", [P, C, G * P], F16) for l in (1, 2)]
        amax = sb("amax", [P, G], F32)
        rmax = sb("rmax", [P, G], F32)

        S4 = ctx.enter_context(nc.psum_tensor("S4", [P, HC, G * C, P], F32))
        S_T = S4[:].rearrange("p h n k -> p (h n) k")
        S = [S_T[:, b * H:(b + 1) * H, :] for b in range(G)]
        bank = [ctx.enter_context(nc.psum_tensor(f"bank{n}", [P, W], F32)) for n in range(4)]
        ps_hT, ps_oT, ps_v, ps_y1 = bank[1], bank[3], bank[0], bank[1]
        ps_q, ps_k, ps_y2, ps_a = bank[2], bank[3], bank[1], bank[3]
        ps_z = [bank[2], bank[1], bank[2]]
        ps_o = [bank[2], bank[0]]

        early_loaded, late_loaded = sem("early_loaded"), sem("late_loaded")
        s_const, ident_ready = sem("pool_constants"), sem("identity_ready")
        s_su = sem("setup_dve")
        deg_summed, deg_powered = sem("deg_summed"), sem("deg_powered")
        norm_rows, adj_turned, norm_turned = sem("norm_rows"), sem("adj_turned"), sem("norm_turned")
        bias_ps, scales_ready, banks_read = sem("bias_in_psum"), sem("scales_ready"), sem("banks_read")
        w_hi_d = sem("w_hi_done")
        maxima_ready, bounds_ready = sem("maxima_ready"), sem("bounds_ready")
        constants = sem("constants_ready")
        x_loaded = [sem(f"x_loaded_{r}") for r in range(PAR)]
        bn_done = [sem(f"bn_done{l}") for l in range(4)]
        mv_done = [sem(f"mv_done{l}") for l in range(4)]
        xb_done = [sem(f"xb_done{l}") for l in range(3)]
        ve_done = [sem(f"ve_done{l}") for l in range(4)]
        rs_done = [sem(f"rs_done{l}") for l in range(4)]
        nm_done = [sem(f"nm_done{l}") for l in range(4)]
        h_done = [sem(f"h_done{l}") for l in range(4)]
        hT_ps, hT_hi_d, hT_lo_d = sem("hT_in_psum"), sem("hT_hi_done"), sem("hT_lo_done")
        q_ps, k_ps, v_ps = sem("q_in_psum"), sem("k_in_psum"), sem("v_in_psum")
        q_hi_d, k_hi_d, v_hi_d = sem("q_hi_done"), sem("k_hi_done"), sem("v_hi_done")
        q_lo_d, k_lo_d, v_lo_d = sem("q_lo_done"), sem("k_lo_done"), sem("v_lo_done")
        s_ps = sem("scores_in_psum")
        sm_d = [sem(f"masked_scores_{b}") for b in range(G)]
        sub_d = [sem(f"max_taken_off_{b}") for b in range(G)]
        sT_ps = [sem(f"scoresT_in_psum_{b}") for b in range(G)]
        ef_d = [sem(f"exp_done_{b}") for b in range(G)]
        eh_d = [sem(f"exp_hi_done_{b}") for b in range(G)]
        el_d = [sem(f"exp_lo_done_{b}") for b in range(G)]
        o_ps = [sem(f"o_in_psum_{b}") for b in range(G)]
        rd_d = [sem(f"rden_done_{b}") for b in range(G)]
        on_d = [sem(f"o_normal_{b}") for b in range(G)]
        oT_ps, oT_hi_d, oT_lo_d = sem("oT_in_psum"), sem("oT_hi_done"), sem("oT_lo_done")
        z_ps = [sem(f"z{l}_in_psum") for l in range(3)]
        x_done = [sem(f"x{l}_done") for l in (1, 2, 3)]
        y_ps = [sem(f"y{l}_in_psum") for l in (1, 2)]
        y_hi_d = [sem(f"y{l}_hi_done") for l in (1, 2)]
        y_lo_d = [sem(f"y{l}_lo_done") for l in (1, 2)]
        a_ps, amax_d, r_d, out_d = (sem(n) for n in ("a_in_psum", "amax_done", "relu_done", "out_done"))
        stored = [sem(f"stored_{r}") for r in range(PAR)]

        def upto(eng, s, i, lag):
            n = i - lag + 1
            if isinstance(n, int):
                n = min(n, NG)
                if n <= 0:
                    return
            eng.wait_ge(s, n)

        def upto_dma(eng, sems, i, lag, par):
            g, r = i - lag, (par - lag) % PAR
            if isinstance(g, int):
                if g >= NG:
                    g -= PAR * ((g - NG) // PAR + 1)
                if g < 0:
                    return
            eng.wait_ge(sems[r], (g - r + 2) * 8)

        def alone(eng, i, *needs):
            if isinstance(i, int):
                for s, lag, *par in needs:
                    (upto_dma if par else upto)(eng, s, i, lag, *par)
                return
            waits = []
            for s, lag, *par in needs:
                r = (par[0] - lag) % PAR if par else None
                n = (i - lag - r + 2) * 8 if par else i - lag + 1
                waits.append((s[r] if par else s, eng.snap(eng.to_reg(n))))
            eng.wait_ge(constants, 1)
            for s, n in waits:
                eng.wait_ge(s, n)

        def live(i, lag):
            return not isinstance(i, int) or 0 <= i - lag < NG

        FIRST = (LAST_LAG + PAR + 1) // PAR * PAR
        END = NG - AHEAD
        LAST = NG + LAST_LAG

        def steps(eng, step, after=()):
            for i in range(FIRST):
                step(i, i % PAR)
                if i < len(after) and after[i]:
                    after[i]()
            with eng.Fori(FIRST, END, PAR) as i:
                for r in range(PAR):
                    step(i + r, r)
            for i in range(END, LAST):
                step(i, i % PAR)

        def flat(ap):
            return ap.rearrange("p c n -> p (c n)")

        block = ctx.enter_context(nc.Block())

        @block.sync
        def _(sp):
            def load(g, par):
                if isinstance(g, int):
                    src, slot = x_g[g:g + 1], X0[:, g % X_RING, :].unsqueeze(1)
                else:
                    src = x_g[bass.ds(nc.s_assert_within(g, 0, NG - 1), 1)]
                    slot = X0[:, bass.ds(g % X_RING, 1), :]
                sp.dma_start(slot.rearrange("p s (b d) -> p (s b) d", b=G),
                             src.rearrange("g p b d -> p (g b) d")).then_inc(x_loaded[par], 16)

            def load_weight(n, s):
                sp.dma_start(w_raw[:, n, :].rearrange("p (c n) -> p c n", c=C),
                             wts[n].rearrange("(c p) n -> p c n", p=P)).then_inc(s, 16)

            load(0, 0)
            sp.dma_start(adj_sb[:], adj).then_inc(early_loaded, 16)
            sp.dma_start(bias_qk[:], bqk[:, 0:2, :]).then_inc(early_loaded, 16)
            for n in (WQ, WK, WV):
                load_weight(n, early_loaded)
            sp.dma_start(bias_v[:], bqk[:, 2, :]).then_inc(late_loaded, 16)
            load_weight(WO, late_loaded)
            sp.wait_ge(s_const, 2)
            sp.dma_start(bias_row[0:1], rows).then_inc(late_loaded, 16)
            for g in range(1, AHEAD):
                load(g, g % PAR)
            for n in (W1, W2):
                load_weight(n, late_loaded)
            sp.dma_start(b3_sb[:], b3).then_inc(late_loaded, 16)

            def step(i, par):
                if live(i, -AHEAD):
                    alone(sp, i, (mv_done[0], 0), (x_done[0], X_RING - AHEAD))
                    load(i + AHEAD, par)
                r = (par - LAST_LAG) % PAR
                if live(i, LAST_LAG):
                    alone(sp, i, (out_d, LAST_LAG))
                    g = i - LAST_LAG
                    dst = out_g[g:g + 1] if isinstance(g, int) else \
                        out_g[bass.ds(nc.s_assert_within(g, 0, NG - 1), 1)]
                    sp.dma_start(dst.rearrange("g p b d -> p (g b) d"),
                                 OUT[r][:].rearrange("p (b d) -> p b d", b=G)).then_inc(stored[r], 16)

            steps(sp, step)
            upto_dma(sp, stored, NG - 1, 0, (NG - 1) % PAR)
            upto_dma(sp, stored, NG - 2, 0, (NG - 2) % PAR)

        @block.tensor
        def _(pe):
            def set_up():
                pe.wait_ge(early_loaded, 16 * 5)
                nc.tensor.transpose(S4[:, 0, 0, :], adj_sb[:], ident[:]).then_inc(adj_turned, 1)
                pe.wait_ge(norm_rows, 1)
                nc.tensor.transpose(S4[:, 1, 0, :], norm_a[:], ident[:]).then_inc(norm_turned, 1)
                pe.wait_ge(late_loaded, 16 * 6)
                pe.wait_ge(s_const, 3)
                for n in range(3):
                    out_ap = S4[:, 2 + n // 2].rearrange("p n k -> p (n k)")[:, n % 2 * D:(n % 2 + 1) * D]
                    if n == 0:
                        for c in range(C):
                            nc.tensor.matmul(out_ap, bv_wide[:, c, :], w_raw[:, WO, c * D:(c + 1) * D],
                                             start=(c == 0), stop=False)
                    mm = nc.tensor.matmul(out_ap, ones[:], bias_row[:, n, :], start=(n > 0), stop=True)
                mm.then_inc(bias_ps, 1)
                pe.wait_ge(banks_read, 2)
                pe.wait_ge(constants, 1)

            def all_constants():
                pe.wait_ge(constants, 2)

            def vacated(i, *tenants):
                for s, task, back in tenants:
                    if live(i - back, LAG[task]):
                        upto(pe, s, i - back, LAG[task])
                        break

            def thrice(out_ap, a, b):
                pairs = [(x_, y_) for c in range(C) for x_, y_ in
                         ((a[0][c], b[0][c]), (a[0][c], b[1][c]), (a[1][c], b[0][c]))]
                for n, (x_, y_) in enumerate(pairs):
                    mm = nc.tensor.matmul(out_ap, x_, y_, start=(n == 0), stop=(n == len(pairs) - 1))
                return mm

            def dense(out_bank, halves, w, s):
                for b in range(G):
                    t = slice(b * P, (b + 1) * P)
                    mm = thrice(out_bank[:, b * D:(b + 1) * D],
                                [[half_[:, c, t] for c in range(C)] for half_ in halves],
                                [[w_[w][:, c, :] for c in range(C)] for w_ in (w_hi, w_lo)])
                mm.then_inc(s, 1)

            def project(out_bank, w, r, s):
                for m in range(C):
                    f = slice(m * P, (m + 1) * P)
                    mm = thrice(out_bank[:, m * G * P:(m + 1) * G * P],
                                [[w_[w][:, c, f] for c in range(C)] for w_ in (w_hi, w_lo)],
                                [[half_[r][:, c, :] for c in range(C)] for half_ in (hT_hi, hT_lo)])
                mm.then_inc(s, 1)

            def turn(out_bank, src, s):
                for b in range(G):
                    for c in range(C):
                        o = c * G * P + b * P
                        mm = nc.tensor.transpose(out_bank[:, o:o + P], src[:, b, c * P:(c + 1) * P], ident[:])
                mm.then_inc(s, 1)

            def mix(out_bank, h, a_t, s):
                for b in range(G):
                    for c in range(C):
                        o = c * G * P + b * P
                        mm = nc.tensor.matmul(out_bank[:, o:o + P], h[:, b, c * P:(c + 1) * P], a_t[:],
                                              start=True, stop=True)
                mm.then_inc(s, 1)

            def scores(i, par, b, m, first, last):
                lag = LAG["s"]
                if not live(i, lag):
                    return
                r = (par - lag) % PAR
                if first:
                    upto(pe, eh_d[0], i, lag + 1)
                    upto(pe, eh_d[1], i, lag + 1)
                    upto(pe, k_lo_d, i, lag)
                    upto(pe, q_lo_d, i, lag)
                t = slice(b * P, (b + 1) * P)
                for n, (q_, k_) in enumerate(((q_hi, k_hi), (q_hi, k_lo), (q_lo, k_hi))):
                    for h in range(HC):
                        f = slice(h * HD, (h + 1) * HD)
                        mm = nc.tensor.matmul(S4[:, h, b * C + m, :], q_[r][f, m, t], k_[r][f, m, t],
                                              start=(n == 0), stop=(n == 2))
                if last:
                    mm.then_inc(s_ps, 1)

            def turn_scores(i, b):
                lag = LAG[f"ts{b}"]
                if live(i, lag):
                    upto(pe, sm_d[1 - b], i, lag)
                    upto(pe, sub_d[b], i, lag)
                    for h in range(H):
                        mm = nc.tensor.transpose(S[b][:, h, :], sm[b][:, h, :], ident[:])
                    mm.then_inc(sT_ps[b], 1)

            def attend(i, par, b, *tenants):
                lag = LAG[f"att{b}"]
                if not live(i, lag):
                    return
                r = (par - lag) % PAR
                vacated(i, *tenants)
                upto(pe, v_lo_d, i, lag)
                upto(pe, eh_d[b], i, lag)
                upto(pe, el_d[b], i, lag)
                for h in range(H):
                    o = h * OC
                    nc.tensor.matmul(ps_o[b][:, o:o + VC], eh[b][:, h, :], v_hi[r][:, b, h, :],
                                     start=True, stop=False)
                    nc.tensor.matmul(ps_o[b][:, o:o + HD], eh[b][:, h, :], v_lo[r][:, b, h, :],
                                     start=False, stop=False)
                    mm = nc.tensor.matmul(ps_o[b][:, o:o + VC], el[b][:, h, :], v_hi[r][:, b, h, :],
                                          start=False, stop=True)
                mm.then_inc(o_ps[b], 1)

            def h_turned(i, par, *tenants):
                lag = LAG["hT"]
                if live(i, lag):
                    vacated(i, *tenants)
                    upto(pe, h_done[0], i, lag)
                    turn(ps_hT, HN[0][(par - lag) % PAR], hT_ps)

            def q_projected(i, par, *tenants):
                lag = LAG["q"]
                if live(i, lag):
                    vacated(i, *tenants)
                    upto(pe, hT_lo_d, i, lag)
                    project(ps_q, WQ, (par - lag) % PAR, q_ps)

            def k_projected(i, par, *tenants):
                lag = LAG["k"]
                if live(i, lag):
                    vacated(i, *tenants)
                    upto(pe, hT_lo_d, i, lag)
                    project(ps_k, WK, (par - lag) % PAR, k_ps)

            def v_projected(i, par, *tenants):
                lag = LAG["v"]
                if live(i, lag):
                    r = (par - lag) % PAR
                    vacated(i, *tenants)
                    upto(pe, hT_lo_d, i, lag)
                    dense(ps_v, (hT_hi[r], hT_lo[r]), WV, v_ps)

            def o_turned(i, par, *tenants):
                lag = LAG["oT"]
                if live(i, lag):
                    vacated(i, *tenants)
                    upto(pe, on_d[0], i, lag)
                    upto(pe, on_d[1], i, lag)
                    turn(ps_oT, on, oT_ps)

            def o_projected(i, par, *tenants):
                lag = LAG["z0"]
                if live(i, lag):
                    vacated(i, *tenants)
                    upto(pe, oT_lo_d, i, lag)
                    dense(ps_z[0], (oT_hi, oT_lo), WO, z_ps[0])

            def h1_mixed(i, par, *tenants):
                lag = LAG["y1"]
                if live(i, lag):
                    vacated(i, *tenants)
                    upto(pe, h_done[1], i, lag)
                    mix(ps_y1, HN[1][(par - lag) % PAR], adj_ts, y_ps[0])

            def y1_projected(i, par, *tenants):
                lag = LAG["z1"]
                if live(i, lag):
                    vacated(i, *tenants)
                    upto(pe, y_lo_d[0], i, lag)
                    dense(ps_z[1], (y_hi[0], y_lo[0]), W1, z_ps[1])

            def h2_mixed(i, par, *tenants):
                lag = LAG["y2"]
                if live(i, lag):
                    vacated(i, *tenants)
                    upto(pe, h_done[2], i, lag)
                    mix(ps_y2, HN[2][(par - lag) % PAR], norm_ts, y_ps[1])

            def y2_projected(i, par, *tenants):
                lag = LAG["z2"]
                if live(i, lag):
                    vacated(i, *tenants)
                    upto(pe, y_lo_d[1], i, lag)
                    dense(ps_z[2], (y_hi[1], y_lo[1]), W2, z_ps[2])

            def layer3(i, par, *tenants):
                lag = LAG["a"]
                if live(i, lag):
                    vacated(i, *tenants)
                    upto(pe, h_done[3], i, lag)
                    nc.tensor.matmul(ps_a[:], adj_t[:], flat(HN[3][(par - lag) % PAR][:]), start=True,
                                     stop=True).then_inc(a_ps, 1)

            def step(i, par):
                h1_mixed(i, par, (y_lo_d[1], "y2", 1), (hT_lo_d, "hT", 1), (x_done[1], "z1", 1),
                         (y_lo_d[0], "y1", 1))
                turn_scores(i, 1)
                y2_projected(i, par, (q_lo_d, "q", 1), (on_d[0], "att0", 1), (x_done[0], "z0", 1),
                             (x_done[2], "z2", 1))
                o_turned(i, par, (k_lo_d, "k", 1), (amax_d, "a", 1), (oT_lo_d, "oT", 1))
                turn_scores(i, 0)
                y1_projected(i, par, (y_lo_d[0], "y1", 0), (y_lo_d[1], "y2", 1),
                             (hT_lo_d, "hT", 1), (x_done[1], "z1", 1))
                o_projected(i, par, (x_done[2], "z2", 0), (q_lo_d, "q", 1), (on_d[0], "att0", 1),
                            (x_done[0], "z0", 1))
                scores(i, par, 0, 0, first=True, last=False)
                h_turned(i, par, (x_done[1], "z1", 0), (y_lo_d[0], "y1", 0), (y_lo_d[1], "y2", 1),
                         (hT_lo_d, "hT", 1))
                scores(i, par, 0, 1, first=False, last=False)
                attend(i, par, 1, (v_lo_d, "v", 1), (on_d[1], "att1", 1))
                attend(i, par, 0, (x_done[0], "z0", 0), (x_done[2], "z2", 0), (q_lo_d, "q", 1),
                       (on_d[0], "att0", 1))
                layer3(i, par, (oT_lo_d, "oT", 0), (k_lo_d, "k", 1), (amax_d, "a", 1))
                scores(i, par, 1, 0, first=False, last=False)
                scores(i, par, 1, 1, first=False, last=True)
                h2_mixed(i, par, (hT_lo_d, "hT", 0), (x_done[1], "z1", 0), (y_lo_d[0], "y1", 0),
                         (y_lo_d[1], "y2", 1))
                q_projected(i, par, (on_d[0], "att0", 0), (x_done[0], "z0", 0),
                            (x_done[2], "z2", 0), (q_lo_d, "q", 1))
                k_projected(i, par, (amax_d, "a", 0), (oT_lo_d, "oT", 0), (k_lo_d, "k", 1))
                v_projected(i, par, (on_d[1], "att1", 0), (v_lo_d, "v", 1))

            pe.wait_ge(ident_ready, 1)
            steps(pe, step, (set_up, None, all_constants))

        @block.vector
        def _(dve):
            count = [0]

            def link(ins):
                count[0] += 1
                ins.then_inc(s_su, 1)
                dve.wait_ge(s_su, count[0])

            v = nc.vector

            def largest(part, n, ap):
                return v.tensor_reduce(bounds[part][:, n:n + 1], ap, X_AXIS, ALU.max,
                                       apply_absolute_value=True)

            def scales(part, biases):
                dve.wait_ge(bounds_ready, part + 1)
                n = 3
                link(v.tensor_scalar(bnd[part][:, 0:n], bound[part][:, 0:n], float(D), TINY, ALU.mult,
                                     ALU.max))
                if biases:
                    link(v.tensor_tensor(bnd[part][:, 0:2], bnd[part][:, 0:2], bound[part][:, n:n + 2],
                                         ALU.add))
                else:
                    link(v.tensor_scalar(bnd[part][:, n:5], bound[part][:, n:5], 2.0 ** -100, None,
                                         ALU.max))
                    n = 5
                link(v.tensor_scalar(pow2[part][:, 0:n].bitcast(I32), bnd[part][:, 0:n].bitcast(I32),
                                     0x7F800000, None, ALU.bitwise_and))
                link(v.reciprocal(up[part][:, 0:n], pow2[part][:, 0:n]))
                v.tensor_scalar(down[part][:, 0:3], pow2[part][:, 0:3], 1.0 / TOP, None, ALU.mult)
                link(v.tensor_scalar(up[part][:, 0:3], up[part][:, 0:3], TOP, None, ALU.mult))
                v.tensor_copy(mark[:, part:part + 1], up[part][:, 0:1]).then_inc(scales_ready, 1)

            def low_weights(part):
                for n in range(3):
                    m = 3 * part + n
                    dve.wait_ge(w_hi_d, m + 1)
                    v.scalar_tensor_tensor(flat(w_lo[m][:]), w_raw[:, m, :], up[part][:, n:n + 1],
                                           flat(w_hi[m][:]), ALU.mult, ALU.subtract)

            def set_up_scores():
                dve.wait_ge(early_loaded, 16 * 5)
                for n in (WQ, WK, WV):
                    largest(0, n, w_raw[:, n, :])
                v.tensor_reduce(bounds[0][:, 3:5], bias_qk[:], X_AXIS, ALU.max,
                                apply_absolute_value=True).then_inc(maxima_ready, 1)
                link(v.tensor_reduce(deg[:, 0:1], adj_sb[:], X_AXIS, ALU.add))
                v.tensor_scalar(deg[:, 1:2], deg[:, 0:1], 0.0, None, ALU.is_gt)
                v.tensor_scalar(deg[:, 2:3], deg[:, 0:1], 1e-37, None, ALU.max).then_inc(deg_summed, 1)
                link(v.tensor_scalar(mask[:], adj_sb[:], 1.0, NEG, ALU.subtract, ALU.mult))
                dve.wait_ge(deg_powered, 1)
                link(v.tensor_tensor(deg[:, 2:3], deg[:, 3:4], deg[:, 1:2], ALU.mult))
                v.tensor_scalar(norm_a[:], adj_sb[:], deg[:, 2:3], None, ALU.mult).then_inc(norm_rows, 1)
                scales(0, True)
                root = float(HD) ** 0.5
                v.scalar_tensor_tensor(scal[:, C_QK:C_QK + 1], down[0][:, WQ:WQ + 1], 1.0 / root,
                                       down[0][:, WK:WK + 1], ALU.mult, ALU.mult)
                link(v.scalar_tensor_tensor(scal[:, C_QK_UP:C_QK_UP + 1], up[0][:, WQ:WQ + 1], root,
                                            up[0][:, WK:WK + 1], ALU.mult, ALU.mult))
                v.tensor_scalar(mask[:], mask[:], scal[:, C_QK_UP:C_QK_UP + 1], None, ALU.mult)
                for n in range(2):
                    v.tensor_scalar(bias_qk_s[:, n, :], bias_qk[:, n, :], up[0][:, n:n + 1], None, ALU.mult)
                dve.wait_ge(norm_turned, 1)
                v.tensor_scalar(norm_t[:], S4[:, 1, 0, :], deg[:, 2:3], None,
                                ALU.mult).then_inc(banks_read, 1)
                low_weights(0)
                v.tensor_copy(mark[:, 2:3], deg[:, 0:1]).then_inc(constants, 1)

            def set_up_maxima():
                dve.wait_ge(late_loaded, 16 * 6)
                dve.wait_ge(banks_read, 2)
                for n in (WO, W1, W2):
                    largest(1, n - 3, w_raw[:, n, :])
                largest(1, 3, adj_sb[:])
                largest(1, 4, norm_t[:]).then_inc(maxima_ready, 1)

            def set_up_rest():
                scales(1, False)
                v.tensor_tensor(scal[:, C_0:C_0 + 1], down[0][:, WV:WV + 1], down[1][:, 0:1], ALU.mult)
                v.tensor_tensor(scal[:, C_1:C_1 + 1], pow2[1][:, 3:4], down[1][:, 1:2], ALU.mult)
                v.tensor_tensor(scal[:, C_2:C_2 + 1], pow2[1][:, 4:5], down[1][:, 2:3], ALU.mult)
                v.tensor_scalar(adj_ts[:], adj_t[:], up[1][:, 3:4], None, ALU.mult)
                v.tensor_scalar(norm_ts[:], norm_t[:], up[1][:, 4:5], None, ALU.mult)
                low_weights(1)
                v.tensor_copy(mark[:, 3:4], deg[:, 0:1]).then_inc(constants, 1)

            def x_in(i, lag):
                g = i - lag
                return X0[:, g % X_RING, :] if isinstance(g, int) else \
                    X0[:, bass.ds(g % X_RING, 1), :].rearrange("p s n -> p (s n)")

            def moments(i, l, par):
                lag = LAG[f"bn{l}"]
                if live(i, lag):
                    if l == 0:
                        upto_dma(dve, x_loaded, i, lag, par)
                        src = x_in(i, lag)
                    else:
                        upto(dve, x_done[l - 1], i, lag)
                        src = XR[l - 1][(par - lag) % PAR]
                    upto(dve, mv_done[l], i, lag + 1)
                    for b in range(G):
                        ins = v.bn_stats(bn[l][:, b, :], src[:, b * D:(b + 1) * D])
                    ins.then_inc(bn_done[l], 1)

            def gathered(i, l, par):
                lag = LAG[f"ag{l}"]
                if live(i, lag):
                    r = (par - lag) % PAR
                    alone(dve, i, (nm_done[l], lag + PAR), (bn_done[l], lag))
                    for b in range(G):
                        ins = v.bn_aggr(mv[l][r][:, b, :], bn[l][:, b, :])
                    ins.then_inc(mv_done[l], 1)

            def variance(i, l, par):
                lag = LAG[f"ve{l}"]
                if live(i, lag):
                    r = (par - lag) % PAR
                    upto(dve, mv_done[l], i, lag)
                    upto(dve, rs_done[l], i, lag + PAR)
                    v.tensor_scalar(veps[l][r][:].unsqueeze(2), mv[l][r][:, :, 1:2], EPS, None,
                                    ALU.add).then_inc(ve_done[l], 1)

            def shift(i, l, par):
                lag = LAG[f"nm{l}"]
                if live(i, lag):
                    r = (par - lag) % PAR
                    upto(dve, rs_done[l], i, lag)
                    upto(dve, h_done[l], i, lag + PAR)
                    v.scalar_tensor_tensor(nmr[l][r][:].unsqueeze(2), mv[l][r][:, :, 0:1], -1.0,
                                           rstd[l][r][:].unsqueeze(2), ALU.mult,
                                           ALU.mult).then_inc(nm_done[l], 1)

            def masked(i, b):
                lag = LAG[f"m{b}"]
                if live(i, lag):
                    alone(dve, i, (s_ps, lag), (sT_ps[b], lag + 1))
                    for h in range(H):
                        ins = v.tensor_tensor_reduce(
                            out=sm[b][:, h, :], in0=S4[:, h % HC, b * C + h // HC, :], in1=mask[:],
                            scale=scal[:, C_QK:C_QK + 1], scalar=LOWEST, op0=ALU.add, op1=ALU.max,
                            accum_out=mx[b][:, h:h + 1])
                    ins.then_inc(sm_d[b], 1)

            def outputs(b):
                return ps_o[b][:, 0:H * OC].rearrange("p (h e) -> p h e", h=H)

            def inverse(i, b):
                lag = LAG[f"rc{b}"]
                if live(i, lag):
                    upto(dve, o_ps[b], i, lag)
                    v.reciprocal(rden[b][:].unsqueeze(2), outputs(b)[:, :, HD:HD + 1]).then_inc(rd_d[b], 1)

            def normal(i, b):
                lag = LAG[f"nt{b}"]
                if live(i, lag):
                    upto(dve, rd_d[b], i, lag)
                    upto(dve, oT_ps, i, lag + 1)
                    v.tensor_tensor(on[:, b, :].rearrange("p (h e) -> p h e", h=H), outputs(b)[:, :, 0:HD],
                                    rden[b][:].unsqueeze(2).broadcast_to([P, H, HD]),
                                    ALU.mult).then_inc(on_d[b], 1)

            def low(i, lag, psum, hi, lo, hi_done, lo_done):
                upto(dve, hi_done, i, lag)
                v.tensor_tensor(lo, psum, hi, ALU.subtract).then_inc(lo_done, 1)

            def low_h(i, par):
                lag = LAG["hTl"]
                if live(i, lag):
                    r = (par - lag) % PAR
                    low(i, lag, ps_hT[:], flat(hT_hi[r][:]), flat(hT_lo[r][:]), hT_hi_d, hT_lo_d)

            def low_o(i):
                lag = LAG["oTl"]
                if live(i, lag):
                    low(i, lag, ps_oT[:], flat(oT_hi[:]), flat(oT_lo[:]), oT_hi_d, oT_lo_d)

            def low_v(i, par):
                lag = LAG["vl"]
                if live(i, lag):
                    r = (par - lag) % PAR
                    low(i, lag, ps_v[:].rearrange("p (g e) -> p g e", e=HD),
                        v_hi[r][:].rearrange("p b h e -> p (b h) e")[:, :, 0:HD],
                        v_lo[r][:].rearrange("p b h e -> p (b h) e"), v_hi_d, v_lo_d)

            def low_y(i, l):
                lag = LAG[f"y{l}l"]
                if live(i, lag):
                    low(i, lag, (ps_y1, ps_y2)[l - 1][:], flat(y_hi[l - 1][:]), flat(y_lo[l - 1][:]),
                        y_hi_d[l - 1], y_lo_d[l - 1])

            def low_biased(i, lag, psum, n, hi, lo, hi_done, lo_done, par):
                if live(i, lag):
                    r = (par - lag) % PAR
                    upto(dve, hi_done, i, lag)
                    for m in range(C):
                        ins = v.scalar_tensor_tensor(
                            lo[r][:, m, :], psum[:, m * G * P:(m + 1) * G * P], bias_qk_s[:, n, m:m + 1],
                            hi[r][:, m, :], ALU.add, ALU.subtract)
                    ins.then_inc(lo_done, 1)

            def low_q(i, par):
                low_biased(i, LAG["ql"], ps_q, 0, q_hi, q_lo, q_hi_d, q_lo_d, par)

            def low_k(i, par):
                low_biased(i, LAG["kl"], ps_k, 1, k_hi, k_lo, k_hi_d, k_lo_d, par)

            def residual(i, l, par):
                lag = LAG[f"r{l}"]
                if live(i, lag):
                    r = (par - lag) % PAR
                    upto(dve, xb_done[l], i, lag)
                    if l < 2:
                        upto(dve, xb_done[l + 1], i, lag + PAR)
                    upto(dve, z_ps[l], i, lag)
                    upto(dve, h_done[l + 1], i, lag + PAR)
                    if l == 2:
                        upto(dve, out_d, i, lag + PAR)
                    v.scalar_tensor_tensor(XR[l][r][:], ps_z[l][:], scal[:, C_0 + l:C_0 + l + 1],
                                           XB[l][r][:].rearrange("p b d -> p (b d)"),
                                           ALU.mult, ALU.add).then_inc(x_done[l], 1)

            def last_max(i):
                lag = LAG["mx"]
                if live(i, lag):
                    upto(dve, a_ps, i, lag)
                    upto(dve, r_d, i, lag + 1)
                    v.tensor_reduce(amax[:], ps_a[:].rearrange("p (b d) -> p b d", b=G), X_AXIS,
                                    ALU.max).then_inc(amax_d, 1)

            def last_relu(i):
                lag = LAG["rm"]
                if live(i, lag):
                    upto(dve, amax_d, i, lag)
                    upto(dve, out_d, i, lag + 1)
                    v.tensor_scalar(rmax[:], amax[:], b3_sb[:, 0:1], 0.0, ALU.add, ALU.max).then_inc(r_d, 1)

            def step(i, par):
                shift(i, 1, par)
                low_y(i, 2)
                masked(i, 0)
                low_q(i, par)
                low_k(i, par)
                low_y(i, 1)
                low_v(i, par)
                residual(i, 2, par)
                moments(i, 0, par)
                low_o(i)
                shift(i, 2, par)
                gathered(i, 0, par)
                shift(i, 3, par)
                moments(i, 3, par)
                residual(i, 1, par)
                shift(i, 0, par)
                gathered(i, 3, par)
                residual(i, 0, par)
                moments(i, 2, par)
                variance(i, 3, par)
                moments(i, 1, par)
                inverse(i, 1)
                low_h(i, par)
                gathered(i, 2, par)
                variance(i, 0, par)
                inverse(i, 0)
                gathered(i, 1, par)
                normal(i, 1)
                variance(i, 1, par)
                last_max(i)
                variance(i, 2, par)
                normal(i, 0)
                last_relu(i)
                masked(i, 1)

            steps(dve, step, (set_up_scores, set_up_maxima, set_up_rest))

        @block.scalar
        def _(act):
            a = nc.scalar

            def apply(i, l, par):
                lag = LAG[f"ap{l}"]
                if live(i, lag):
                    r = (par - lag) % PAR
                    g = i - lag
                    if l > 0:
                        src = XR[l - 1][r]
                    elif isinstance(g, int):
                        src = X0[:, g % X_RING, :]
                    else:
                        src = X0[:, bass.ds(g % X_RING, 1), :].rearrange("p s n -> p (s n)")
                    upto(act, nm_done[l], i, lag)
                    upto(act, (hT_ps, y_ps[0], y_ps[1], a_ps)[l], i, lag + PAR)
                    for b in range(G):
                        ins = a.activation(HN[l][r][:, b, :], src[:, b * D:(b + 1) * D], ACT.Relu,
                                           bias=nmr[l][r][:, b:b + 1], scale=rstd[l][r][:, b:b + 1])
                    ins.then_inc(h_done[l], 1)

            def high(i, lag, in_psum, psum, hi, hi_done, used, used_lag):
                upto(act, in_psum, i, lag)
                upto(act, used, i, used_lag)
                a.activation(hi, psum, ACT.Copy).then_inc(hi_done, 1)

            def high_h(i, par):
                lag = LAG["hTh"]
                if live(i, lag):
                    high(i, lag, hT_ps, ps_hT[:], flat(hT_hi[(par - lag) % PAR][:]), hT_hi_d,
                         v_ps, lag + PAR)

            def high_o(i):
                lag = LAG["oTh"]
                if live(i, lag):
                    high(i, lag, oT_ps, ps_oT[:], flat(oT_hi[:]), oT_hi_d, z_ps[0], lag + 1)

            def high_v(i, par):
                lag = LAG["vh"]
                if live(i, lag):
                    high(i, lag, v_ps, ps_v[:].rearrange("p (g e) -> p g e", e=HD),
                         v_hi[(par - lag) % PAR][:].rearrange("p b h e -> p (b h) e")[:, :, 0:HD],
                         v_hi_d, o_ps[0], lag + PAR)

            def high_y(i, l):
                lag = LAG[f"y{l}h"]
                if live(i, lag):
                    high(i, lag, y_ps[l - 1], (ps_y1, ps_y2)[l - 1][:], flat(y_hi[l - 1][:]),
                         y_hi_d[l - 1], z_ps[l], lag + 1)

            def high_biased(i, lag, in_psum, psum, n, hi, hi_done, par):
                if live(i, lag):
                    r = (par - lag) % PAR
                    upto(act, in_psum, i, lag)
                    upto(act, s_ps, i, lag + PAR)
                    for m in range(C):
                        ins = a.activation(hi[r][:, m, :], psum[:, m * G * P:(m + 1) * G * P], ACT.Identity,
                                           bias=bias_qk_s[:, n, m:m + 1])
                    ins.then_inc(hi_done, 1)

            def high_q(i, par):
                high_biased(i, LAG["qh"], q_ps, ps_q, 0, q_hi, q_hi_d, par)

            def high_k(i, par):
                high_biased(i, LAG["kh"], k_ps, ps_k, 1, k_hi, k_hi_d, par)

            def exponentials(i, b):
                lag = LAG[f"ex{b}"]
                if live(i, lag):
                    upto(act, sT_ps[b], i, lag)
                    upto(act, el_d[b], i, lag + 1)
                    a.activation(ef[b][:], S[b], ACT.Exp).then_inc(ef_d[b], 1)
                    upto(act, o_ps[b], i, lag + 1)
                    a.activation(eh[b][:], S[b], ACT.Exp).then_inc(eh_d[b], 1)

            def last_sum(i, par):
                lag = LAG["last"]
                if live(i, lag):
                    r = (par - lag) % PAR
                    upto(act, r_d, i, lag)
                    upto_dma(act, stored, i, lag + PAR, par)
                    for b in range(G):
                        ins = a.activation(OUT[r][:, b * D:(b + 1) * D], XR[2][r][:, b * D:(b + 1) * D],
                                           ACT.Identity, bias=rmax[:, b:b + 1])
                    ins.then_inc(out_d, 1)

            def high_weights(part):
                act.wait_ge(scales_ready, part + 1)
                for n in range(3):
                    m = 3 * part + n
                    a.activation(flat(w_hi[m][:]), w_raw[:, m, :], ACT.Copy,
                                 scale=up[part][:, n:n + 1]).then_inc(w_hi_d, 1)

            def set_up_scores():
                act.wait_ge(early_loaded, 16 * 5)
                high_weights(0)
                act.wait_ge(adj_turned, 1)
                act.wait_ge(bias_ps, 1)
                a.activation(adj_t[:], S4[:, 0, 0, :], ACT.Copy)
                for n in range(3):
                    ins = a.activation(
                        bias[:, n, :],
                        S4[:, 2 + n // 2].rearrange("p n k -> p (n k)")[:, n % 2 * D:(n % 2 + 1) * D],
                        ACT.Copy)
                ins.then_inc(banks_read, 1)
                act.wait_ge(s_const, 4)
                act.wait_ge(constants, 1)

            def set_up_rest():
                act.wait_ge(late_loaded, 16 * 6)
                high_weights(1)

            def step(i, par):
                high_q(i, par)
                apply(i, 1, par)
                high_k(i, par)
                high_y(i, 1)
                high_v(i, par)
                exponentials(i, 1)
                high_o(i)
                exponentials(i, 0)
                apply(i, 3, par)
                apply(i, 2, par)
                high_h(i, par)
                apply(i, 0, par)
                high_y(i, 2)
                last_sum(i, par)

            act.wait_ge(ident_ready, 1)
            a.activation(table_in[:], ident[:, 0:1], ACT.Exp)
            steps(act, step, (set_up_scores, None, set_up_rest))

        @block.gpsimd
        def _(pool):
            g_ = nc.gpsimd
            g_.memset(ident[:], 0.0).then_inc(s_const, 1)
            pool.wait_ge(s_const, 1)
            g_.affine_select(out=ident[:], in_=ident[:], compare_op=ALU.not_equal, fill=1.0, base=0,
                             pattern=[[-1, P]], channel_multiplier=1).then_inc(ident_ready, 1)
            g_.memset(half[:], -0.5)
            g_.memset(ones[:], 1.0)
            g_.memset(bias_row[:], 0.0).then_inc(s_const, 1)

            def powers(i, l, par):
                lag = LAG[f"pw{l}"]
                if live(i, lag):
                    r = (par - lag) % PAR
                    upto(pool, ve_done[l], i, lag)
                    upto(pool, h_done[l], i, lag + PAR)
                    g_.tensor_tensor(rstd[l][r][:], veps[l][r][:], half[:], ALU.pow).then_inc(rs_done[l], 1)

            def set_up_scores():
                pool.wait_ge(maxima_ready, 1)
                g_.partition_all_reduce(bound[0][:], bounds[0][:], P, RMAX).then_inc(bounds_ready, 1)
                pool.wait_ge(deg_summed, 1)
                g_.tensor_tensor(deg[:, 3:4], deg[:, 2:3], half[:, 0:1], ALU.pow).then_inc(deg_powered, 1)
                pool.wait_ge(late_loaded, 16 * 6)
                pool.wait_ge(s_const, 2)
                for c in range(C):
                    ins = g_.tensor_scalar(bv_wide[:, c, :], ones[:], bias_v[:, c:c + 1], 0.0, ALU.mult,
                                           ALU.add)
                ins.then_inc(s_const, 1)
                for r in range(PAR):
                    ins = g_.memset(v_hi[r][:], 1.0)
                ins.then_inc(s_const, 1)

            def set_up_rest():
                pool.wait_ge(maxima_ready, 2)
                g_.partition_all_reduce(bound[1][:], bounds[1][:], P, RMAX).then_inc(bounds_ready, 1)
                pool.wait_ge(banks_read, 2)

            def biased(i, l, par):
                lag = LAG[f"xb{l}"]
                if live(i, lag):
                    r = (par - lag) % PAR
                    g = i - lag
                    needs = ((bn_done[0] if l == 0 else x_done[l - 1], lag), (x_done[l], lag + PAR))
                    if l > 0:
                        for s, need_lag in needs:
                            upto(pool, s, i, need_lag)
                        src = XR[l - 1][r][:]
                    else:
                        alone(pool, i, *needs)
                        src = X0[:, g % X_RING, :] if isinstance(g, int) else \
                            X0[:, bass.ds(g % X_RING, 1), :].rearrange("p s n -> p (s n)")
                    g_.tensor_tensor(XB[l][r][:], src.rearrange("p (b d) -> p b d", b=G),
                                     bias[:, l, :].unsqueeze(1).broadcast_to([P, G, D]),
                                     ALU.add).then_inc(xb_done[l], 1)

            def less_max(i, b):
                lag = LAG[f"lm{b}"]
                if live(i, lag):
                    upto(pool, sm_d[b], i, lag)
                    g_.tensor_tensor(sm[b][:], sm[b][:], mx[b][:].unsqueeze(2).broadcast_to([P, H, P]),
                                     ALU.subtract).then_inc(sub_d[b], 1)

            def exp_low(i, b):
                lag = LAG[f"el{b}"]
                if live(i, lag):
                    upto(pool, eh_d[b], i, lag)
                    upto(pool, ef_d[b], i, lag)
                    upto(pool, o_ps[b], i, lag + 1)
                    g_.tensor_tensor(el[b][:], ef[b][:], eh[b][:], ALU.subtract).then_inc(el_d[b], 1)

            def step(i, par):
                powers(i, 0, par)
                less_max(i, 1)
                less_max(i, 0)
                powers(i, 2, par)
                exp_low(i, 1)
                exp_low(i, 0)
                biased(i, 1, par)
                biased(i, 2, par)
                powers(i, 1, par)
                powers(i, 3, par)
                biased(i, 0, par)

            pool.wait_ge(s_const, 2)
            steps(pool, step, (set_up_scores, set_up_rest))


def kernel(**inputs):
    import numpy as _np
    import concourse.bacc as _bacc
    from concourse import mybir as _mybir
    from concourse.bass_utils import run_bass_kernel_spmd as _run

    a = {k: _np.ascontiguousarray(v) for k, v in inputs.items()}
    col = lambda b: b.reshape(C, P).T
    arrays = {"x": a["x"], "adj": a["adj"]}
    for n, k in zip(WEIGHTS, ("L0_gnn_Wq", "L0_gnn_Wk", "L0_gnn_Wv", "L0_gnn_Wo", "L1_gnn_weight",
                              "L2_gnn_weight")):
        arrays[f"w_{n}"] = a[k]
    arrays["bias_cols"] = _np.ascontiguousarray(
        _np.stack([col(a["L0_gnn_bq"]), col(a["L0_gnn_bk"]), col(a["L0_gnn_bv"])], axis=1))
    arrays["bias_3"] = _np.ascontiguousarray(a["L3_gnn_b"].reshape(P, 1))
    arrays["bias_rows"] = _np.ascontiguousarray(
        _np.stack([a["L0_gnn_bo"], a["L1_gnn_bias"], a["L2_gnn_bias"]])[None])
    nc = _bacc.Bacc("TRN2", target_bir_lowering=False, num_devices=1)
    ap = {k: nc.dram_tensor(f"in_{k}", v.shape, _mybir.dt.from_np(v.dtype), kind="ExternalInput").ap()
          for k, v in arrays.items()}
    out = nc.dram_tensor("out_0", a["x"].shape, _mybir.dt.from_np(a["x"].dtype), kind="ExternalOutput").ap()
    build(nc, ap["x"], ap["adj"], [ap[f"w_{n}"] for n in WEIGHTS], ap["bias_cols"], ap["bias_3"],
          ap["bias_rows"], out)
    r = _run(nc, [{f"in_{k}": v for k, v in arrays.items()}], core_ids=[0])
    return r.results[0]["out_0"]
```
